# Optimizing a Trainium2 kernel written in Bass

```python
import numpy as np
import jax
import jax.numpy as jnp

def _softmax(x, axis=-1):
    return jax.nn.softmax(x, axis=axis)

def _gelu(x):
    return jax.nn.gelu(x, approximate=True)

def _silu(x):
    return jax.nn.silu(x)

def _sigmoid(x):
    return jax.nn.sigmoid(x)

def _layernorm(x, axis=-1, eps=1e-05):
    m = jnp.mean(x, axis=axis, keepdims=True)
    v = jnp.var(x, axis=axis, keepdims=True)
    return (x - m) / jnp.sqrt(v + eps)

def _scatter_add(tgt, idx, src, axis=0):
    return tgt.at[idx].add(src)

def _segment_sum(src, seg, n):
    return jax.ops.segment_sum(src, seg, n)
kernel_name = 'mk_cond_resid_d2_seqx_r4_114e7a'

def setup_inputs(seed: int=0):
    np.random.seed(seed)
    _w = jnp.asarray

    def _rec_inputs():
        import jax
        import jax.numpy as jnp
        _rk = jax.random.key(seed)
        x = -0.0003929 + 0.9999 * jax.random.normal(jax.random.fold_in(_rk, 1), (2, 1024, 256), jnp.float32)
        _lenS = 1024 - jax.random.randint(jax.random.fold_in(_rk, 7), (2,), 0, max(1, 1024 // 4) + 1, jnp.int32)
        _lenS2 = 1024 - jax.random.randint(jax.random.fold_in(_rk, 8), (2,), 0, max(1, 1024 // 4) + 1, jnp.int32)
        cond_1024 = 0.00513981 + 1.0024 * jax.random.normal(jax.random.fold_in(_rk, 11), (2, 256), jnp.float32)
        _validS = jnp.arange(1024)[None, :] < _lenS[:, None]
        _validS2 = jnp.arange(1024)[None, :] < _lenS2[:, None]
        _causal = jnp.tril(jnp.ones((1024, 1024), dtype=bool))
        mask_Bx1x1xS_ff0 = jnp.where(jnp.ones((2, 1, 1, 1024), dtype=bool), 0.0, -1000000000.0).astype(jnp.float32)
        return (x, cond_1024, mask_Bx1x1xS_ff0)
    x, cond_1024, mask_Bx1x1xS_ff0 = _rec_inputs()

    def _L0_cond_setup():
        import jax, jax.numpy as jnp
        import numpy as np
        D = 256
        H = 256
        key = jax.random.key(seed)
        k1, k2, k3, k4 = jax.random.split(key, 4)
        x = jax.random.normal(k1, (32, 128, D), dtype=jnp.float32)
        h0 = jax.random.normal(k2, (32, H), dtype=jnp.float32)
        Wx = jax.random.normal(k3, (D, 4 * H), dtype=jnp.float32) / jnp.sqrt(float(D))
        Wh = jax.random.normal(k4, (H, 4 * H), dtype=jnp.float32) / jnp.sqrt(float(H))
        b = jnp.zeros((4 * H,), dtype=jnp.float32)
        return {'x': x, 'h0': h0, 'Wx': Wx, 'Wh': Wh, 'b': b}
    _L0_cond_all = _L0_cond_setup()
    _L0_cond_in = {k: v for k, v in _L0_cond_all.items() if k in ('Wx', 'Wh', 'b')}
    del _L0_cond_all

    def _L1_cond_setup():
        import jax, jax.numpy as jnp
        import numpy as np
        EMBED = 256
        HEADS = 16
        HDIM = EMBED // HEADS
        MASK_OUT = -10000.0

        def _split_heads(t):
            B, T, _ = t.shape
            return t.reshape(B, T, HEADS, HDIM).transpose(0, 2, 1, 3)
        key = jax.random.key(seed)
        ks = jax.random.split(key, 12)
        B, S = (4, 1023)
        scale = 0.02
        return {'word_hidden_states': jax.random.normal(ks[0], (B, S, EMBED), jnp.float32), 'image_hidden_states': jax.random.normal(ks[1], (B, EMBED), jnp.float32), 'attention_mask': jnp.zeros((B, 1, 1, S), jnp.float32), 'c_attn_w': jax.random.normal(ks[2], (EMBED, 3 * EMBED), jnp.float32) * scale, 'c_attn_b': jnp.zeros((3 * EMBED,), jnp.float32), 'c_proj_w': jax.random.normal(ks[3], (EMBED, EMBED), jnp.float32) * scale, 'c_proj_b': jnp.zeros((EMBED,), jnp.float32), 'uk_w': jax.random.normal(ks[4], (EMBED, EMBED), jnp.float32) * scale, 'uk_b': jnp.zeros((EMBED,), jnp.float32), 'uv_w': jax.random.normal(ks[5], (EMBED, EMBED), jnp.float32) * scale, 'uv_b': jnp.zeros((EMBED,), jnp.float32)}
    _L1_cond_all = _L1_cond_setup()
    _L1_cond_in = {k: v for k, v in _L1_cond_all.items() if k in ('c_attn_w', 'c_attn_b', 'c_proj_w', 'c_proj_b', 'uk_w', 'uk_b', 'uv_w', 'uv_b')}
    del _L1_cond_all
    return {'x': x, 'cond_1024': cond_1024, 'mask_Bx1x1xS_ff0': mask_Bx1x1xS_ff0, 'L0_cond_Wx': _L0_cond_in['Wx'], 'L0_cond_Wh': _L0_cond_in['Wh'], 'L0_cond_b': _L0_cond_in['b'], 'L1_cond_c_attn_w': _L1_cond_in['c_attn_w'], 'L1_cond_c_attn_b': _L1_cond_in['c_attn_b'], 'L1_cond_c_proj_w': _L1_cond_in['c_proj_w'], 'L1_cond_c_proj_b': _L1_cond_in['c_proj_b'], 'L1_cond_uk_w': _L1_cond_in['uk_w'], 'L1_cond_uk_b': _L1_cond_in['uk_b'], 'L1_cond_uv_w': _L1_cond_in['uv_w'], 'L1_cond_uv_b': _L1_cond_in['uv_b']}

def reference(x, cond_1024, mask_Bx1x1xS_ff0, L0_cond_Wx, L0_cond_Wh, L0_cond_b, L1_cond_c_attn_w, L1_cond_c_attn_b, L1_cond_c_proj_w, L1_cond_c_proj_b, L1_cond_uk_w, L1_cond_uk_b, L1_cond_uv_w, L1_cond_uv_b):
    import jax
    import jax.numpy as jnp

    def _L0_cond_ref(x, h0, Wx, Wh, b):
        import jax, jax.numpy as jnp
        import numpy as np
        D = 256
        H = 256
        Hdim = h0.shape[1]
        x_proj = jnp.einsum('ntd,df->ntf', x, Wx) + b

        def step(carry, xp_t):
            prev_h, prev_c = carry
            h_bar = xp_t + prev_h @ Wh
            i = jax.nn.sigmoid(h_bar[:, 0:Hdim])
            f = jax.nn.sigmoid(h_bar[:, Hdim:2 * Hdim])
            o = jax.nn.sigmoid(h_bar[:, 2 * Hdim:3 * Hdim])
            g = jnp.tanh(h_bar[:, 3 * Hdim:4 * Hdim])
            next_c = f * prev_c + i * g
            next_h = o * jnp.tanh(next_c)
            return ((next_h, next_c), next_h)
        c0 = jnp.zeros_like(h0)
        xs = jnp.swapaxes(x_proj, 0, 1)
        _, hs = jax.lax.scan(step, (h0, c0), xs)
        return jnp.swapaxes(hs, 0, 1)

    def _L1_cond_ref(word_hidden_states, image_hidden_states, attention_mask, c_attn_w, c_attn_b, c_proj_w, c_proj_b, uk_w, uk_b, uv_w, uv_b):
        import jax, jax.numpy as jnp
        import numpy as np
        EMBED = 256
        HEADS = 16
        HDIM = EMBED // HEADS
        MASK_OUT = -10000.0

        def _split_heads(t):
            B, T, _ = t.shape
            return t.reshape(B, T, HEADS, HDIM).transpose(0, 2, 1, 3)
        B, S, _ = word_hidden_states.shape
        qkv = word_hidden_states @ c_attn_w + c_attn_b
        q_word, k_word, v_word = jnp.split(qkv, 3, axis=-1)
        img = image_hidden_states[:, None, :]
        k_img = img @ uk_w.T + uk_b
        v_img = img @ uv_w.T + uv_b
        k = jnp.concatenate([k_img, k_word], axis=1)
        v = jnp.concatenate([v_img, v_word], axis=1)
        q = _split_heads(q_word)
        k = _split_heads(k)
        v = _split_heads(v)
        scores = jnp.einsum('bhqd,bhkd->bhqk', q, k) / jnp.sqrt(jnp.float32(HDIM))
        qi = jnp.arange(S)[:, None]
        kj = jnp.arange(S + 1)[None, :]
        causal = kj <= qi + 1
        scores = jnp.where(causal[None, None], scores, jnp.float32(MASK_OUT))
        zero_col = jnp.zeros(attention_mask.shape[:-1] + (1,), attention_mask.dtype)
        mask = jnp.concatenate([zero_col, attention_mask], axis=-1)
        scores = scores + mask
        attn = jax.nn.softmax(scores, axis=-1)
        out = jnp.einsum('bhqk,bhkd->bhqd', attn, v)
        out = out.transpose(0, 2, 1, 3).reshape(B, S, EMBED)
        out = out @ c_proj_w + c_proj_b
        return out
    x = x + _L0_cond_ref(x, cond_1024, L0_cond_Wx, L0_cond_Wh, L0_cond_b)
    x = x + _L1_cond_ref(x, cond_1024, mask_Bx1x1xS_ff0, L1_cond_c_attn_w, L1_cond_c_attn_b, L1_cond_c_proj_w, L1_cond_c_proj_b, L1_cond_uk_w, L1_cond_uk_b, L1_cond_uv_w, L1_cond_uv_b)
    return x

_drawn_inputs = setup_inputs


def setup_inputs(seed=0):
    import zlib

    import numpy as np

    out = dict(_drawn_inputs(seed))
    spreads = {'L0_cond_b': (0.0, 0.1),
     'L1_cond_c_attn_b': (0.0, 0.1),
     'L1_cond_c_proj_b': (0.0, 0.334),
     'L1_cond_uk_b': (0.0, 0.8),
     'L1_cond_uv_b': (0.0, 0.8)}
    factors = {'cond_1024': 8.0, 'L1_cond_c_attn_w': 6.804, 'L1_cond_uk_w': 8.0, 'L1_cond_uv_w': 8.0}
    for name, (base, spread) in spreads.items():
        noise = np.random.default_rng([zlib.crc32(name.encode()), seed]).standard_normal(out[name].shape)
        drawn = base * np.exp(spread * noise) if base else spread * noise
        out[name] = jnp.asarray(drawn.astype(out[name].dtype))
    for name, factor in factors.items():
        out[name] = (out[name] * factor).astype(out[name].dtype)
    return out
```

```python
from contextlib import ExitStack

import concourse.bass as bass
from concourse import mybir

F32 = mybir.dt.float32
BF16 = mybir.dt.bfloat16
ALU = mybir.AluOpType
ACT = mybir.ActivationFunctionType
AX = mybir.AxisListType.X

P = 128
BATCH, SEQ, D = 2, 1024, 256
HEADS, HDIM = 16, 16
KT = D // P
QUADS = 4
LANES = 32
GATES = 4
HALF = GATES * LANES
STEPS = 16
BLOCK = P
PHASES = SEQ // BLOCK
BODIES = BLOCK // STEPS
TILES = HEADS // QUADS
ROWS = STEPS // 2 * BATCH
CHUNK = 4
XCH = P // BATCH
MASK_ROW, MAX_ROW = HDIM, HDIM + 1
NEG = -1e30
SCALE = HDIM ** -0.5


def lstm_attention(nc, x_t, wx, wh, b_x, h0, w_qk, b_qk, w_v, b_v, w_p, b_p, w_uk, b_uk, w_uv, b_uv,
                   mask, ident_in, sel_in, tri_in, tri_t_in, head_col, head_row, out):
    ctx = ExitStack()
    with ctx:
        def sb(name, shape, dt=F32):
            return ctx.enter_context(nc.sbuf_tensor(name, shape, dt))

        def bank(name):
            return ctx.enter_context(nc.psum_tensor(name, [P, 512], F32))

        def sem(name):
            return ctx.enter_context(nc.semaphore(name))

        xp_dram = nc.dram_tensor("gate_inputs", (SEQ * BATCH, GATES * D), F32, kind="Internal").ap()

        xT = sb("xT", [P, KT, SEQ, BATCH])
        Wx = sb("Wx", [P, KT, GATES * D])
        Wh = sb("Wh", [P, KT, GATES * D])
        bx = sb("bx", [P, GATES * D])
        condT = sb("condT", [P, KT, BATCH])
        cond4 = sb("cond4", [P, KT, BATCH, QUADS])
        Wqk = sb("Wqk", [P, TILES, 2, KT, P])
        Bqk = sb("Bqk", [2, TILES, 2, P])
        Wv = sb("Wv", [P, KT, TILES, P])
        Bv = sb("Bv", [1, TILES, P])
        Wp = sb("Wp", [P, TILES, D])
        bp = sb("bp", [P, D])
        Wuk = sb("Wuk", [P, KT, TILES, P])
        Buk = sb("Buk", [1, TILES, P])
        Wuv = sb("Wuv", [P, KT, TILES, P])
        Buv = sb("Buv", [1, TILES, P])
        ones_mask = sb("ones_mask", [2, BATCH, SEQ])
        ident = sb("ident", [P, P])
        identh = sb("identh", [P, P], BF16)
        sel = sb("sel", [P, P])
        tri = sb("tri", [P, P])
        tri_t = sb("tri_t", [P, P])
        tri_th = sb("tri_th", [P, P], BF16)
        headc = sb("headc", [P, QUADS])
        headr = sb("headr", [QUADS, P])
        xp_st = [sb(f"xp_st{i}", [P, GATES * D]) for i in range(2)]
        Tsb = [sb(f"gates_t{b}", [P, HALF]) for b in range(KT)]
        G = [sb(f"gates{b}", [P, 2, GATES * BATCH + BATCH]) for b in range(KT)]
        UV = [sb(f"uv{b}", [P, 2 * BATCH]) for b in range(KT)]
        TC = [sb(f"tanh_c{b}", [P, BATCH]) for b in range(KT)]
        ring = sb("h2_ring", [P, STEPS, KT, BATCH])
        X1 = [sb(f"x1_{i}", [P, KT, BATCH, BLOCK]) for i in range(2)]
        xps = sb("xps", [P, 2, 512])
        kv_all = sb("kv_all", [P, BODIES, SEQ + PHASES * P])
        KIMG = sb("KIMG", [P, BODIES, QUADS])
        kimg = sb("kimg", [P, BODIES])
        VIMG = sb("VIMG", [QUADS, BODIES, P])
        wst = sb("wst", [P, 2, KT, P])
        bst = sb("bst", [2, 2, P])
        x1st = sb("x1st", [P, KT, BLOCK])
        kst = sb("kst", [P, SEQ])
        vst = sb("vst", [P, PHASES, P])
        kimg_st = sb("kimg_st", [P, QUADS])
        vimg_st = sb("vimg_st", [QUADS, P])
        qT = sb("qT", [P, BLOCK])
        qaug = sb("qaug", [P, BLOCK])
        mx = sb("mx", [P, QUADS, 4])
        MT = sb("MT", [P, P])
        junk = sb("junk", [P, QUADS, P])
        PT = sb("PT", [P, QUADS, PHASES, BLOCK])
        PTi = sb("PTi", [QUADS, BLOCK])
        oT = sb("oT", [P, BLOCK])
        rec = sb("rec", [P, BLOCK])
        OT = sb("OT", [P, BLOCK])
        OUT = [sb(f"out_rows{i}", [P, BATCH, D]) for i in range(2)]

        gp = [bank(f"gates_ps{b}") for b in range(KT)]
        S = [bank(f"scores_ps{j}") for j in range(QUADS)]
        PV = bank("pv_ps")
        misc = bank("misc_ps")

        def sems(text):
            return [sem(name) for name in text.split()]

        loaded, ones_set, scaled, ready = sems("loaded ones_set weights_scaled prologue_done")
        xp_mm, xp_add, img_mm, img_copied, img_made = sems("xp_mm xp_add img_mm img_copied img_made")
        xp_out = [sem(f"xp_out{i}") for i in range(2)]
        xp_in = [sem(f"gate_inputs_in{i}") for i in range(2)]
        x1_evac, wst_in, x1st_in, kst_in, vst_in, k_stored, out_stored = sems(
            "x1_evac wst_in x1st_in kst_in vst_in k_stored out_stored")
        bst_ready, kimg_ready, vimg_ready, vimg_used = sems("bst_ready kimg_ready vimg_ready vimg_used")
        misc_ready, misc_free = sems("misc_ready misc_free")
        p1_ready, p2_ready, exp_done = [[sem(f"{name}_{c}") for c in range(2)]
                                        for name in ("scores_ready", "scores_t_ready", "exp_done")]
        max0_done, max_done, mt_done, pv_ready, oT_ready, OT_ready = sems(
            "max0_done max_done mt_done pv_ready oT_ready OT_ready")
        g_ready, t_done, th_done, uv_done, c_done, tc_done, h_done = [
            [sem(f"{name}{b}") for b in range(KT)]
            for name in ("g_ready", "t_done", "th_done", "uv_done", "c_done", "tc_done", "h_done")]

        block = ctx.enter_context(nc.Block())

        LOADS = [(xT, x_t), (Wx, wx), (Wh, wh), (condT, h0), (Wqk, w_qk), (Bqk, b_qk), (Wv, w_v),
                 (Bv, b_v), (Wp, w_p), (Wuk, w_uk), (Buk, b_uk), (Wuv, w_uv), (Buv, b_uv),
                 (ident, ident_in), (sel, sel_in), (tri, tri_in), (tri_t, tri_t_in),
                 (headc, head_col), (headr, head_row)]
        N_LOAD = 16 * (len(LOADS) + 3)
        XPN = 2 * SEQ // XCH

        def inner(n):
            return 0 if isinstance(n, int) else 1

        def tiles_before(ph, n):
            return BODIES * (ph - 1) + n

        def late_tiles_before(ph, n):
            return BODIES * (ph - 1 - CHUNK) + n

        def wait(eng, semaphore, count):
            if not (isinstance(count, int) and count <= 0):
                eng.wait_ge(semaphore, count)

        def misc_use(ph, n, new, old, name):
            first = not inner(n)
            names = (["q", "k", "img1", "v"] + ["init"] * first + ["max"]) * new + ["sel"] * old + ["img2"] * new + ["proj"] * old
            before = 8 * tiles_before(ph, n) + (ph - 1) + inner(n) - 2 * (not (ph == 1 and first))
            return before + names.index(name)

        def chunks(blocks):
            return [(c, min(CHUNK, blocks - c)) for c in range(0, blocks, CHUNK)]

        def wait_exps(eng, ph, n):
            if (ph if inner(n) else ph - 1) > CHUNK:
                eng.wait_ge(exp_done[1], late_tiles_before(ph, n))
            else:
                wait(eng, exp_done[0], tiles_before(ph, n))

        def bodies(eng, body):
            with eng.Fori(0, BODIES) as n:
                body(0, n, 1, 0, 0)
            for ph in range(1, PHASES + 1):
                body(ph, 0, int(ph < PHASES), 1, int(ph > 1))
                with eng.Fori(1, BODIES) as n:
                    body(ph, n, int(ph < PHASES), 1, 1)
            body(PHASES + 1, 0, 0, 0, 1)

        @block.sync
        def _(sp):
            for dst, source in LOADS:
                sp.dma_start(dst[:], source).then_inc(loaded, 16)
            sp.dma_start(bx[:, :], b_x.partition_broadcast(P)).then_inc(loaded, 16)
            sp.dma_start(bp[:, :], b_p.partition_broadcast(P)).then_inc(loaded, 16)
            sp.wait_ge(ones_set, 1)
            sp.dma_start(ones_mask[1:2, :, :], mask).then_inc(loaded, 16)
            for c in range(XPN):
                sp.wait_ge(xp_add, c + 1)
                sp.dma_start(xp_dram[c // 2 * P:(c // 2 + 1) * P, c % 2 * 512:(c % 2 + 1) * 512],
                             xps[:, c % 2, :]).then_inc(xp_out[c % 2], 16)
            for half in range(2):
                sp.wait_ge(xp_out[half], 16 * (XPN // 2))
            sp.wait_ge(ready, 1)
            for half in range(2):
                sp.dma_start(xp_st[half][0:ROWS, :], xp_dram[half * ROWS:(half + 1) * ROWS, :]).then_inc(xp_in[half], 16)
            sp.wait_ge(loaded, N_LOAD)
            sp.dma_start(wst[:], Wqk[:, 0]).then_inc(wst_in, 16)

            def body(ph, n, lstm, new, old):
                t = BLOCK * ph + STEPS * n
                T = tiles_before(ph, n)
                cur, B = (ph - 1) % 2, ph
                row = sp.snap((t + STEPS) % SEQ * BATCH) if lstm else None
                batch, next_tile = (sp.snap(n // TILES), sp.snap((n + 1) % TILES)) if inner(n) else (0, 1)
                if new:
                    sp.wait_ge(x1_evac, 2 * BODIES * ph)
                    sp.dma_start(x1st[:], X1[cur][:, :, batch, :]).then_inc(x1st_in, 16)
                    if B > 1:
                        if not inner(n):
                            sp.wait_ge(k_stored, 16 * T)
                        if (B if inner(n) else B - 1) > CHUNK:
                            sp.wait_ge(p2_ready[1], late_tiles_before(ph, n))
                        else:
                            sp.wait_ge(p2_ready[0], T)
                        sp.dma_start(kst[:, 0:(B - 1) * BLOCK], kv_all[:, n, 0:(B - 1) * BLOCK]).then_inc(kst_in, 16)
                    if B < PHASES:
                        sp.wait_ge(misc_free, misc_use(ph, n, new, old, "k") + 1)
                        sp.dma_start(kv_all[:, n, (B - 1) * BLOCK:B * BLOCK],
                                     kst[:, (B - 1) * BLOCK:B * BLOCK]).then_inc(k_stored, 16)
                    sp.wait_ge(misc_ready, misc_use(ph, n, new, old, "k") + 1)
                    sp.dma_start(wst[:], Wqk[:, next_tile]).then_inc(wst_in, 16)
                if lstm:
                    sp.wait_ge(g_ready[1], t + STEPS // 2)
                    sp.dma_start(xp_st[0][0:ROWS, :], xp_dram[bass.ds(row, ROWS), :]).then_inc(xp_in[0], 16)
                if new:
                    sp.wait_ge(misc_free, misc_use(ph, n, new, old, "v") + 1)
                    wait(sp, pv_ready, T)
                    sp.dma_start(vst[:, 0:B, :].rearrange("p k m -> p (k m)"),
                                 kv_all[:, n, SEQ:SEQ + B * P]).then_inc(vst_in, 16)
                if lstm:
                    sp.wait_ge(g_ready[1], t + STEPS)
                    sp.dma_start(xp_st[1][0:ROWS, :], xp_dram[bass.ds(row + ROWS, ROWS), :]).then_inc(xp_in[1], 16)
                if old and not inner(n):
                    i = ph - 2
                    sp.wait_ge(misc_free, misc_use(ph, n, new, old, "proj") + 1)
                    for b in range(BATCH):
                        sp.dma_start(out[b, i * BLOCK:(i + 1) * BLOCK, :], OUT[i % 2][:, b, :]).then_inc(out_stored, 16)

            bodies(sp, body)
            sp.wait_ge(out_stored, 16 * BATCH * PHASES)
            sp.wait_ge(wst_in, 16 * (BODIES * PHASES + 1))

        @block.gpsimd
        def _(pool):
            nc.gpsimd.memset(ones_mask[:], 1.0).then_inc(ones_set, 1)
            pool.wait_ge(loaded, N_LOAD)
            pool.wait_ge(img_made, 2)
            nc.gpsimd.tensor_copy(bst[:], Bqk[:, 0]).then_inc(bst_ready, 1)
            nc.gpsimd.tensor_copy(kimg_st[:], KIMG[:, 0]).then_inc(kimg_ready, 1)

            def body(ph, n, lstm, new, old):
                if not new:
                    return
                pool.wait_ge(misc_ready, misc_use(ph, n, new, old, "k") + 1)
                nc.gpsimd.tensor_copy(bst[:], Bqk[:, (n + 1) % TILES]).then_inc(bst_ready, 1)
                wait(pool, vimg_used, tiles_before(ph, n))
                nc.gpsimd.tensor_copy(vimg_st[:], VIMG[:, n]).then_inc(vimg_ready, 1)
                pool.wait_ge(misc_ready, misc_use(ph, n, new, old, "img2") + 1)
                nc.gpsimd.tensor_copy(kimg_st[:], KIMG[:, (n + 1) % BODIES]).then_inc(kimg_ready, 1)

            bodies(pool, body)

        @block.tensor
        def _(pe):
            mm = nc.tensor.matmul

            def group(b, lhsT, rhs, start, stop):
                for j in range(QUADS):
                    lo = j * D + b * HALF
                    last = mm(gp[b][LANES * j:LANES * j + BATCH, 0:HALF], lhsT, rhs[:, lo:lo + HALF],
                              start=start, stop=stop, skip_group_check=True, tile_position=(0, LANES * j))
                return last

            def inject(step):
                half, k = divmod(step, STEPS // 2)
                for b in range(KT):
                    group(b, ident[:, BATCH * k:BATCH * k + BATCH], xp_st[half], True, False)

            pe.wait_ge(scaled, 1)
            for c in range(XPN):
                if c >= QUADS:
                    pe.wait_ge(xp_add, c - QUADS + 1)
                for k in range(KT):
                    last = mm(S[c % QUADS][:, :],
                              xT[:, k, c // 2 * XCH:(c // 2 + 1) * XCH, :].rearrange("p t b -> p (t b)"),
                              Wx[:, k, c % 2 * 512:(c % 2 + 1) * 512], start=k == 0, stop=k == KT - 1)
                last.then_inc(xp_mm, 1)
            pe.wait_ge(ready, 1)
            for tile in range(TILES):
                o = misc[:, BATCH * tile:BATCH * tile + BATCH]
                for k in range(KT):
                    mm(o, Wuk[:, k, tile, :], condT[:, k, :], start=k == 0, stop=False, skip_group_check=True)
                last = mm(o, Buk[:, tile, :], ones_mask[0:1, 0, 0:BATCH], start=False, stop=True, skip_group_check=True)
            last.then_inc(img_mm, 1)
            pe.wait_ge(xp_add, XPN)
            for b in range(BATCH):
                for k in range(KT):
                    mm(S[b][0:QUADS, :], cond4[:, k, b, :], Wuv[:, k].rearrange("p t m -> p (t m)"), start=k == 0, stop=False)
                last = mm(S[b][0:QUADS, :], ones_mask[0:1, 0, 0:QUADS], Buv[:].rearrange("p t m -> p (t m)"), start=False, stop=True)
            last.then_inc(img_mm, 1)
            pe.wait_ge(img_made, 2)
            pe.wait_ge(xp_in[0], 16)
            inject(0)

            def body(ph, n, lstm, new, old):
                t = BLOCK * ph + STEPS * n
                T = tiles_before(ph, n)
                cur, B = (ph - 1) % 2, ph
                Bold = ph if inner(n) else ph - 1
                mask_at = (B - 1) * BLOCK

                def open_misc(name):
                    wait(pe, misc_free, misc_use(ph, n, new, old, name))

                def quad(j):
                    return slice(LANES * j, LANES * (j + 1))

                def scores_t(c, blocks, total):
                    for kb in blocks:
                        col = (kb - c) * BLOCK
                        for j in range(QUADS):
                            last = mm(S[j][:, col:col + BLOCK], kst[quad(j), kb * BLOCK:(kb + 1) * BLOCK],
                                      qaug[quad(j), :], start=True, stop=kb != total - 1,
                                      skip_group_check=True, tile_position=(LANES * j, 0))
                        if kb == total - 1:
                            for j in range(QUADS):
                                last = mm(S[j][:, col:col + BLOCK], identh[:, :], tri_th[:, :], start=False,
                                          stop=True, skip_group_check=True)
                    return last

                def values(blocks, total):
                    for kb in blocks:
                        for j in range(QUADS):
                            last = mm(PV[quad(j), 0:BLOCK], vst[:, kb, quad(j)], PT[:, j, kb, :],
                                      start=False, stop=kb == total - 1, skip_group_check=True,
                                      tile_position=(0, LANES * j))
                    return last

                for st in range(STEPS):
                    if lstm:
                        for k in range(KT):
                            pe.wait_ge(h_done[k], t + st + 1)
                            for b in range(KT):
                                last = group(b, ring[:, (st - 1) % STEPS, k, :], Wh[:, k], False, k == KT - 1)
                                if k == KT - 1:
                                    last.then_inc(g_ready[b], 1)
                    if st == 0 and old and Bold > CHUNK + 2:
                        scores_t(CHUNK, range(CHUNK + 2, Bold), Bold).then_inc(p2_ready[1], 1)
                    if st in (1, 2) and new:
                        open_misc("q" if st == 1 else "k")
                        if st == 1:
                            pe.wait_ge(wst_in, 16 * (T + 1))
                            pe.wait_ge(bst_ready, T + 1)
                            pe.wait_ge(x1_evac, 2 * BODIES * ph)
                        for k in range(KT):
                            mm(misc[:, 0:BLOCK], wst[:, st - 1, k, :], X1[cur][:, k, n // TILES, :], start=k == 0, stop=False)
                        mm(misc[:, 0:BLOCK], bst[:, st - 1, :], ones_mask[:, n // TILES, mask_at:mask_at + BLOCK],
                           start=False, stop=True).then_inc(misc_ready, 1)
                    if st == 3 and new:
                        open_misc("img1")
                        pe.wait_ge(kimg_ready, T + 1)
                        mm(misc[:, 0:QUADS], qT[:, :], kimg_st[:, :], start=True, stop=True).then_inc(misc_ready, 1)
                        if B > 1:
                            pe.wait_ge(kst_in, 16 * (T - BODIES + 1))
                        wait_exps(pe, ph, n)
                    if new and (st == 3 or (st == 7 and B > CHUNK)):
                        half = int(st == 7)
                        c, nb = chunks(B)[half]
                        if half:
                            pe.wait_ge(max0_done, late_tiles_before(ph, n) + 1)
                        for j in range(QUADS):
                            last = mm(S[j][:, 0:nb * BLOCK], qT[quad(j), :], kst[quad(j), c * BLOCK:(c + nb) * BLOCK],
                                      start=True, stop=True, tile_position=(LANES * j, 0))
                        last.then_inc(p1_ready[half], 1)
                    if st == 4 and new:
                        open_misc("v")
                        pe.wait_ge(x1st_in, 16 * (T + 1))
                        for k in range(KT):
                            mm(misc[:, 0:P], x1st[:, k, :], Wv[:, k, n % TILES, :], start=k == 0, stop=False)
                        mm(misc[:, 0:P], ones_mask[0:1, 0, 0:BLOCK], Bv[:, n % TILES, :], start=False,
                           stop=True).then_inc(misc_ready, 1)
                    if st == 5 and new and not inner(n):
                        open_misc("init")
                        for b in range(BATCH):
                            for k in range(KT):
                                lo = b * D + k * P
                                last = nc.tensor.transpose(misc[:, lo:lo + P], X1[cur][:, k, b, :], ident[:, :])
                        last.then_inc(misc_ready, 1)
                    if old and st in (5, 6, 8, 9):
                        lo = {5: 0, 6: 2, 8: 4, 9: 6}[st]
                        some = range(lo, min(lo + 2, Bold))
                        if st == 5:
                            pe.wait_ge(vimg_ready, T)
                            mm(PV[:, 0:BLOCK], vimg_st[:, :], PTi[:, :], start=True, stop=False,
                               skip_group_check=True).then_inc(vimg_used, 1)
                            pe.wait_ge(exp_done[0], T)
                            pe.wait_ge(vst_in, 16 * T)
                        if st == 8 and some:
                            pe.wait_ge(exp_done[1], late_tiles_before(ph, n))
                        if some:
                            last = values(some, Bold)
                            if some[-1] == Bold - 1:
                                last.then_inc(pv_ready, 1)
                    if st == 11 and new:
                        open_misc("max")
                        pe.wait_ge(mt_done, T + 1)
                        nc.tensor.transpose(misc[:, 0:P], MT[:, :], ident[:, :]).then_inc(misc_ready, 1)
                    if st == 12 and old:
                        open_misc("sel")
                        pe.wait_ge(oT_ready, T)
                        mm(misc[:, 0:BLOCK], sel[:, :], oT[:, :], start=True, stop=True).then_inc(misc_ready, 1)
                    if new and st in (12, 13):
                        if st == 12:
                            pe.wait_ge(misc_free, misc_use(ph, n, new, old, "max") + 1)
                        nb = min(CHUNK, B)
                        some = range(0, min(2, nb)) if st == 12 else range(2, nb)
                        if some:
                            last = scores_t(0, some, B)
                            if some[-1] == nb - 1:
                                last.then_inc(p2_ready[0], 1)
                    if st == 14 and new:
                        open_misc("img2")
                        mm(misc[0:QUADS, 0:BLOCK], kimg_st[:, :], qaug[:, :], start=True,
                           stop=True).then_inc(misc_ready, 1)
                    if new and st == 15 and B > CHUNK:
                        pe.wait_ge(exp_done[0], T + 1)
                        last = scores_t(CHUNK, range(CHUNK, min(CHUNK + 2, B)), B)
                        if B <= CHUNK + 2:
                            last.then_inc(p2_ready[1], 1)
                    if st == 15 and old:
                        open_misc("proj")
                        pe.wait_ge(OT_ready, T)
                        tile = (n - 1) % TILES if inner(n) else TILES - 1
                        mm(misc[:, 0:D], OT[:, :], Wp[:, tile, :], start=True, stop=True).then_inc(misc_ready, 1)
                    if lstm:
                        nxt = (st + 1) % STEPS
                        if nxt == 0:
                            pe.wait_ge(xp_in[0], 16 * (BODIES * ph + n + 2))
                        if nxt == STEPS // 2:
                            pe.wait_ge(xp_in[1], 16 * (BODIES * ph + n + 1))
                        for b in range(KT):
                            pe.wait_ge(t_done[b], t + st + 1)
                        inject(nxt)

            bodies(pe, body)

        @block.scalar
        def _(act):
            act.wait_ge(ready, 1)
            nc.scalar.activation(TC[0][:, :], condT[:, 0, :], ACT.Tanh)
            act.wait_ge(img_mm, 1)
            nc.scalar.activation(kimg[:, :].rearrange("p (b t) -> p t b", b=BATCH),
                                 misc[:, 0:BODIES].rearrange("p (t b) -> p t b", b=BATCH), ACT.Copy).then_inc(img_copied, 1)

            def body(ph, n, lstm, new, old):
                t = BLOCK * ph + STEPS * n
                T = tiles_before(ph, n)
                B = ph
                Bold = ph if inner(n) else ph - 1

                def exps(c, total, heads):
                    nb = min(CHUNK, total - c)
                    for j in heads:
                        last = nc.scalar.activation(PT[:, j, c:c + nb, :].rearrange("p k q -> p (k q)"),
                                                    S[j][:, 0:nb * BLOCK], ACT.Exp)
                    if heads[-1] == QUADS - 1:
                        last.then_inc(exp_done[c // CHUNK], 1)

                for st in range(STEPS):
                    now, nxt = st % 2, (st + 1) % 2
                    if lstm:
                        for b in range(KT):
                            act.wait_ge(t_done[b], t + st + 1)
                            nc.scalar.activation(
                                G[b][:, now, 0:GATES * BATCH].rearrange("p (g r) -> p g r", r=BATCH),
                                Tsb[b][:, :].rearrange("p (g r) -> p g r", g=GATES)[:, :, 0:BATCH],
                                ACT.Tanh).then_inc(th_done[b], 1)
                        for b in range(KT):
                            act.wait_ge(c_done[b], t + st + 1)
                            nc.scalar.activation(TC[b][:, :], G[b][:, nxt, GATES * BATCH:], ACT.Tanh,
                                                 scale=0.5).then_inc(tc_done[b], 1)
                    if st in (0, 1) and old and Bold > CHUNK:
                        if st == 0:
                            act.wait_ge(p2_ready[1], late_tiles_before(ph, n))
                        exps(CHUNK, Bold, (0, 1) if st == 0 else (2, 3))
                    if st == 1 and new:
                        act.wait_ge(misc_ready, misc_use(ph, n, new, old, "q") + 1)
                        nc.scalar.activation(qT[:, :], misc[:, 0:BLOCK], ACT.Copy, scale=SCALE).then_inc(misc_free, 1)
                    if st == 2 and new:
                        act.wait_ge(misc_ready, misc_use(ph, n, new, old, "k") + 1)
                        wait(act, k_stored, 16 * T if B < PHASES else 16 * BODIES * (PHASES - 1))
                        nc.scalar.activation(kst[:, (B - 1) * BLOCK:B * BLOCK], misc[:, 0:BLOCK],
                                             ACT.Copy).then_inc(misc_free, 1)
                    if st == 4 and new:
                        act.wait_ge(misc_ready, misc_use(ph, n, new, old, "v") + 1)
                        nc.scalar.activation(kv_all[:, n, SEQ + (B - 1) * P:SEQ + B * P], misc[:, 0:P], ACT.Copy).then_inc(misc_free, 1)
                    if st == 9 and old:
                        act.wait_ge(pv_ready, T)
                        nc.scalar.activation(oT[:, :], PV[:, 0:BLOCK], ACT.Copy).then_inc(oT_ready, 1)
                    if st in (13, 14) and new:
                        if st == 13:
                            act.wait_ge(p2_ready[0], T + 1)
                        exps(0, B, (0, 1) if st == 13 else (2, 3))
                    if st == 14 and new:
                        act.wait_ge(misc_ready, misc_use(ph, n, new, old, "img2") + 1)
                        nc.scalar.activation(PTi[:, :], misc[0:QUADS, 0:BLOCK], ACT.Exp).then_inc(misc_free, 1)

            bodies(act, body)

        @block.vector
        def _(dve):
            v = nc.vector
            dve.wait_ge(loaded, N_LOAD)
            for w, of_sigmoids, of_tanh in ((Wx, 0.5, None), (Wh, 0.25, 0.5)):
                gates = w[:].rearrange("p k (m g c) -> p (k m) g c", g=GATES, c=LANES)
                v.tensor_scalar(gates[:, :, 0:3, :], gates[:, :, 0:3, :], of_sigmoids, None, ALU.mult)
                if of_tanh:
                    v.tensor_scalar(gates[:, :, 3, :], gates[:, :, 3, :], of_tanh, None, ALU.mult)
            gates = bx[:, :].rearrange("p (m g c) -> p m g c", g=GATES, c=LANES)
            v.tensor_scalar(gates[:, :, 0:3, :], gates[:, :, 0:3, :], 0.5, None, ALU.mult).then_inc(scaled, 1)
            for b in range(KT):
                v.memset(xp_st[b][:, :], 0.0)
                v.memset(gp[b][:, :], 0.0)
                v.memset(G[b][:, 0, GATES * BATCH:], 0.0)
            v.memset(MT[:, :], 0.0)
            v.tensor_copy(identh[:, :], ident[:, :])
            v.tensor_copy(tri_th[:, :], tri_t[:, :])
            for r in range(QUADS):
                v.tensor_copy(cond4[:, :, :, r], condT[:, :, :])
            for k in range(KT):
                v.tensor_scalar(ring[:, STEPS - 1, k, :], condT[:, k, :], 2.0, None, ALU.mult).then_inc(h_done[k], 1)
            v.memset(UV[0][:, :], 0.0).then_inc(ready, 1)
            dve.wait_ge(scaled, 1)
            for c in range(XPN):
                dve.wait_ge(xp_mm, c + 1)
                if c >= 2:
                    dve.wait_ge(xp_out[c % 2], 16 * (c // 2))
                v.tensor_tensor(xps[:, c % 2, :], S[c % QUADS][:, :], bx[:, c % 2 * 512:(c % 2 + 1) * 512],
                                ALU.add).then_inc(xp_add, 1)
            dve.wait_ge(img_copied, 1)
            v.tensor_tensor(KIMG[:, :, :], kimg[:, :].unsqueeze(2).to_broadcast([P, BODIES, QUADS]),
                            headc[:, :].unsqueeze(1).to_broadcast([P, BODIES, QUADS]), ALU.mult).then_inc(img_made, 1)
            dve.wait_ge(img_mm, 2)
            for b in range(BATCH):
                last = v.tensor_tensor(VIMG[:, b * TILES:(b + 1) * TILES, :],
                                       S[b][0:QUADS, :].rearrange("p (t m) -> p t m", t=TILES),
                                       headr[:, :].unsqueeze(1).to_broadcast([QUADS, TILES, P]), ALU.mult)
            last.then_inc(img_made, 1)

            def body(ph, n, lstm, new, old):
                t = BLOCK * ph + STEPS * n
                T = tiles_before(ph, n)
                cur, B = (ph - 1) % 2, ph

                def maxima(c, j):
                    full = min(CHUNK, B - 1 - c)
                    if full > 0:
                        last = v.reduce_max(mx[:, j, 2 + c // CHUNK:3 + c // CHUNK], S[j][:, 0:full * BLOCK], AX)
                    if full < CHUNK:
                        last = v.tensor_tensor_reduce(out=junk[:, j, :], in0=S[j][:, full * BLOCK:(full + 1) * BLOCK],
                                                      in1=tri[:, :], scale=1.0, scalar=NEG, op0=ALU.add, op1=ALU.max,
                                                      accum_out=mx[:, j, 1:2])
                    return last

                for st in range(STEPS):
                    now, nxt = st % 2, (st + 1) % 2
                    if lstm:
                        for b in range(KT):
                            dve.wait_ge(g_ready[b], t + st + 1)
                            v.transpose(Tsb[b][:, :], gp[b][:, 0:HALF]).then_inc(t_done[b], 1)
                        for b in range(KT):
                            dve.wait_ge(th_done[b], t + st + 1)
                            v.scalar_tensor_tensor(UV[b][:, :], G[b][:, now, 0:4], 1.0, G[b][:, now, 6:10],
                                                   ALU.add, ALU.mult).then_inc(uv_done[b], 1)
                            dve.wait_ge(uv_done[b], t + st + 1)
                            v.scalar_tensor_tensor(G[b][:, nxt, 8:10], UV[b][:, 2:4], 0.5, UV[b][:, 0:2],
                                                   ALU.mult, ALU.add).then_inc(c_done[b], 1)
                        for b in range(KT):
                            dve.wait_ge(tc_done[b], t + st + 1)
                            v.scalar_tensor_tensor(ring[:, st, b, :], G[b][:, now, 4:6], 1.0, TC[b][:, :],
                                                   ALU.add, ALU.mult).then_inc(h_done[b], 1)
                    if st == 3 and new:
                        dve.wait_ge(p1_ready[0], T + 1)
                        dve.wait_ge(misc_ready, misc_use(ph, n, new, old, "img1") + 1)
                        v.tensor_copy(mx[:, :, 0], misc[:, 0:QUADS]).then_inc(misc_free, 1)
                    if st in (3, 4, 5, 6) and new:
                        last = maxima(0, st - 3)
                        if st == 6 and B > CHUNK:
                            last.then_inc(max0_done, 1)
                        elif st == 6:
                            last.then_inc(max_done, 1)
                    if st == 5 and new and not inner(n):
                        dve.wait_ge(misc_ready, misc_use(ph, n, new, old, "init") + 1)
                        wait(dve, out_stored, 16 * BATCH * (ph - 2))
                        v.tensor_tensor(OUT[cur][:, :, :], misc[:, :].rearrange("p (b f) -> p b f", b=BATCH),
                                        bp[:, :].unsqueeze(1).to_broadcast([P, BATCH, D]), ALU.add).then_inc(misc_free, 1)
                    if st == 7 and new and B > CHUNK:
                        dve.wait_ge(p1_ready[1], late_tiles_before(ph, n) + 1)
                    if lstm and st in (7, 15):
                        half = int(st == 15)
                        at = t + half * STEPS // 2
                        where = STEPS * n + half * STEPS // 2
                        for k in range(KT):
                            dve.wait_ge(h_done[k], at + STEPS // 2 + 1)
                        for b in range(BATCH):
                            last = v.scalar_tensor_tensor(
                                X1[ph % 2][:, :, b, bass.ds(where, STEPS // 2)],
                                ring[:, half * STEPS // 2:(half + 1) * STEPS // 2, :, b].rearrange("p t k -> p k t"), 0.5,
                                xT[:, :, bass.ds(at, STEPS // 2), b], ALU.mult, ALU.add)
                        last.then_inc(x1_evac, 1)
                    if st in (7, 8, 9, 10) and new and B > CHUNK:
                        last = maxima(CHUNK, st - 7)
                        if st == 10:
                            last.then_inc(max_done, 1)
                    if st == 10 and new:
                        dve.wait_ge(max_done, T + 1)
                        parts = 2 + (B > 1) + (B > CHUNK + 1)
                        v.tensor_reduce(MT[:, MAX_ROW::LANES], mx[:, :, 0:parts], AX, ALU.max,
                                        negate=True).then_inc(mt_done, 1)
                    if st == 11 and new:
                        dve.wait_ge(misc_ready, misc_use(ph, n, new, old, "max") + 1)
                        v.tensor_tensor(qaug[:, :], qT[:, :], misc[:, 0:BLOCK], ALU.add).then_inc(misc_free, 1)
                    if st == 12 and old:
                        dve.wait_ge(misc_ready, misc_use(ph, n, new, old, "sel") + 1)
                        v.reciprocal(rec[:, 0:BLOCK // 2], misc[:, 0:BLOCK // 2])
                    if st == 13 and old:
                        v.reciprocal(rec[:, BLOCK // 2:], misc[:, BLOCK // 2:BLOCK]).then_inc(misc_free, 1)
                    if st == 14 and old:
                        dve.wait_ge(misc_free, misc_use(ph, n, new, old, "sel") + 1)
                        v.tensor_tensor(OT[:, :], oT[:, :], rec[:, :], ALU.mult).then_inc(OT_ready, 1)
                    if st == 15 and old:
                        o = OUT[cur][:, (n - 1) // TILES, :] if inner(n) else OUT[1 - cur][:, BATCH - 1, :]
                        dve.wait_ge(misc_ready, misc_use(ph, n, new, old, "proj") + 1)
                        v.tensor_tensor(o, o, misc[:, 0:D], ALU.add).then_inc(misc_free, 1)

            bodies(dve, body)


def _positions():
    import numpy as np
    feature = np.array([[64 * (q // 32) + 32 * k + q % 32 for q in range(128)] for k in range(2)])
    column = np.array([256 * g + 64 * j + 32 * b + p for j in range(4) for b in range(2) for g in range(4) for p in range(32)])
    return feature, column


def kernel(**inputs):
    import numpy as np
    import concourse.bacc as _bacc
    from concourse import mybir as _mybir
    from concourse.bass_utils import run_bass_kernel_spmd as _run

    g = {k: np.asarray(v) for k, v in inputs.items()}
    feature, column = _positions()

    def by_feature(w):
        return w[feature].transpose(1, 0, *range(2, w.ndim + 1))

    def in_slots(w, ones=()):
        w = w.reshape(*w.shape[:-1], TILES, QUADS, HDIM)
        padded = np.zeros((*w.shape[:-1], LANES), np.float32)
        padded[..., :HDIM] = w
        for at, value in ones:
            padded[..., at] = value
        return padded.reshape(*w.shape[:-3], TILES, P)

    c_w, c_b = g["L1_cond_c_attn_w"], g["L1_cond_c_attn_b"]
    w_qk = np.stack([in_slots(by_feature(c_w[:, i * D:(i + 1) * D])) for i in range(2)], 1)
    b_q = in_slots(c_b[0:D], [(MASK_ROW, 1 / SCALE)])
    b_k = in_slots(c_b[D:2 * D], [(MAX_ROW, 1.0)])
    mask_slot = in_slots(np.zeros(D, np.float32), [(MASK_ROW, 1.0)])
    b_qk = np.stack([np.stack([b_q, b_k], 1), np.stack([np.zeros_like(b_q), mask_slot], 1)])
    rows = in_slots(np.ascontiguousarray(g["L1_cond_c_proj_w"].T)).transpose(2, 1, 0)
    block = np.arange(P) // LANES
    arrays = {
        "x_t": by_feature(g["x"].transpose(2, 1, 0)),
        "wx": by_feature(g["L0_cond_Wx"][:, column]),
        "wh": by_feature(g["L0_cond_Wh"][:, column]),
        "b_x": g["L0_cond_b"][column],
        "h0": by_feature(g["cond_1024"].T),
        "w_qk": w_qk.transpose(0, 3, 1, 2, 4),
        "b_qk": b_qk,
        "w_v": in_slots(by_feature(c_w[:, 2 * D:])),
        "b_v": in_slots(c_b[2 * D:], [(HDIM, 1.0)])[None],
        "w_p": rows[:, :, feature.reshape(-1)],
        "b_p": g["L1_cond_c_proj_b"][feature.reshape(-1)],
        "w_uk": in_slots(by_feature(g["L1_cond_uk_w"].T)),
        "b_uk": in_slots(g["L1_cond_uk_b"], [(MAX_ROW, 1.0)])[None],
        "w_uv": in_slots(by_feature(g["L1_cond_uv_w"].T)),
        "b_uv": in_slots(g["L1_cond_uv_b"], [(HDIM, 1.0)])[None],
        "mask": g["mask_Bx1x1xS_ff0"].reshape(1, BATCH, SEQ),
        "ident_in": np.eye(P, dtype=np.float32),
        "sel_in": ((np.arange(P)[:, None] % LANES == HDIM) & (block[:, None] == block)).astype(np.float32),
        "tri_in": np.where(np.arange(P)[None] > np.arange(P)[:, None], np.float32(NEG), np.float32(0)),
        "tri_t_in": np.where(np.arange(P)[:, None] > np.arange(P)[None], np.float32(NEG), np.float32(0)),
        "head_col": (block[:, None] == np.arange(QUADS)).astype(np.float32),
        "head_row": (np.arange(QUADS)[:, None] == block).astype(np.float32),
    }
    arrays = {k: np.ascontiguousarray(v) for k, v in arrays.items()}
    nc = _bacc.Bacc("TRN2", target_bir_lowering=False, num_devices=1)
    args = {k: nc.dram_tensor(k, v.shape, _mybir.dt.float32, kind="ExternalInput").ap() for k, v in arrays.items()}
    out = nc.dram_tensor("out", (BATCH, SEQ, D), _mybir.dt.float32, kind="ExternalOutput").ap()
    lstm_attention(nc, **args, out=out)
    r = _run(nc, [arrays], core_ids=[0])
    rows = r.results[0]["out"]
    return rows.reshape(BATCH, SEQ, KT, QUADS, LANES).transpose(0, 1, 3, 2, 4).reshape(BATCH, SEQ, D)
```

```python
from contextlib import ExitStack

import concourse.bass as bass
from concourse import mybir

F32 = mybir.dt.float32
F32R = mybir.dt.float32r
BF16 = mybir.dt.bfloat16
ALU = mybir.AluOpType
ACT = mybir.ActivationFunctionType
AX = mybir.AxisListType.X

P = 128
BATCH, SEQ, D = 2, 1024, 256
HEADS, HDIM = 16, 16
KT = D // P
QUADS = 4
LANES = 32
GATES = 4
HALF = GATES * LANES
STEPS = 16
BLOCK = P
PHASES = SEQ // BLOCK
BODIES = BLOCK // STEPS
TILES = HEADS // QUADS
ROWS = STEPS // 2 * BATCH
PARTS = 3
CHUNK = 4
XCH = P // BATCH
PIECE = 256
PIECES = GATES * D // PIECE
MASK_ROW, MAX_ROW = HDIM, HDIM + 1
NEG = -1e30
ONES_AT, C_AT = GATES, 7
SCALE = HDIM ** -0.5


def lstm_attention(nc, x_t, wx, wh, b_x, h0, w_qk, b_qk, w_v, b_v, w_p, b_p, w_uk, b_uk, w_uv, b_uv,
                   mask, ident_in, pick_in, sel_in, tri_in, tri_t_in, head_col, head_row, out):
    ctx = ExitStack()
    with ctx:
        def sb(name, shape, dt=F32):
            return ctx.enter_context(nc.sbuf_tensor(name, shape, dt))

        def bank(name):
            return ctx.enter_context(nc.psum_tensor(name, [P, 512], F32))

        def sem(name):
            return ctx.enter_context(nc.semaphore(name))

        xp_dram = nc.dram_tensor("gate_inputs", (SEQ * BATCH // ROWS, PARTS, ROWS, GATES * D), BF16,
                                 kind="Internal").ap()

        xT = sb("xT", [P, KT, SEQ, BATCH])
        Wx = sb("Wx", [P, KT, GATES * D])
        Wh = sb("Wh", [P, KT, GATES * D])
        bx = sb("bx", [P, GATES * D])
        condT = sb("condT", [P, KT, BATCH])
        cond4 = sb("cond4", [P, KT, BATCH, QUADS])
        Wqk = sb("Wqk", [P, TILES, 2, KT, P])
        Bqk = sb("Bqk", [2, TILES, 2, P])
        Wv = sb("Wv", [P, KT, TILES, P])
        Bv = sb("Bv", [1, TILES, P])
        Wp = sb("Wp", [P, TILES, D])
        bp = sb("bp", [P, D])
        Buk = sb("Buk", [1, TILES, P])
        Buv = sb("Buv", [1, TILES, P])
        ones_mask = sb("ones_mask", [2, BATCH, SEQ])
        ident = sb("ident", [P, P])
        identh = sb("identh", [P, P], BF16)
        sel = sb("sel", [P, P])
        tri = sb("tri", [P, P])
        tri_t = sb("tri_t", [P, P])
        tri_th = sb("tri_th", [P, P], BF16)
        headc = sb("headc", [P, QUADS])
        headr = sb("headr", [QUADS, P])
        xp_st = [sb(f"xp_st{i}", [P, GATES * D], BF16) for i in range(2)]
        pick = sb("pick_rows", [P, ROWS], BF16)
        pickf = sb("pick_rows_f32", [P, ROWS])
        zero = sb("zero", [P, 1])
        x_st = sb("x_st", [P, KT, XCH * BATCH])
        Tsb = [sb(f"gates_t{b}", [P, HALF]) for b in range(KT)]
        G = [sb(f"gates{b}", [P, 2, BATCH, 8]) for b in range(KT)]
        products = [sb(f"products{b}", [P, BATCH, 4]) for b in range(KT)]
        TC = [sb(f"tanh_c{b}", [P, BATCH]) for b in range(KT)]
        ring = sb("h2_ring", [P, STEPS, KT, BATCH])
        X1 = [sb(f"x1_{i}", [P, KT, BATCH, BLOCK]) for i in range(2)]
        xps = sb("xps", [P, GATES * D])
        xp_parts = sb("xp_parts", [P, PARTS, GATES * D], BF16)
        kv_all = sb("kv_all", [P, BODIES, SEQ + PHASES * P])
        KIMG = sb("KIMG", [P, BODIES, QUADS])
        kimg = sb("kimg", [P, BODIES])
        VIMG = sb("VIMG", [QUADS, BODIES, P])
        wst = sb("wst", [P, 2, KT, P])
        bst = sb("bst", [2, 2, P])
        x1st = sb("x1st", [P, KT, BLOCK])
        kst = sb("kst", [P, SEQ])
        vst = sb("vst", [P, PHASES, P])
        Wuk = kst[:, :].rearrange("p (k t m) -> p k t m", k=KT, t=TILES)
        Wuv = vst[:, :, :].rearrange("p (k t) m -> p k t m", k=KT)
        kimg_st = sb("kimg_st", [P, QUADS])
        vimg_st = sb("vimg_st", [QUADS, P])
        qT = sb("qT", [P, BLOCK])
        q_r = sb("q_rounded", [P, BLOCK], F32R)
        k_r = sb("k_rounded", [P, SEQ], F32R)
        qaug = sb("qaug", [P, BLOCK])
        mx = sb("mx", [P, QUADS, 4])
        MT = sb("MT", [P, P])
        junk = sb("junk", [P, QUADS, P])
        PT = sb("PT", [P, QUADS, PHASES, BLOCK])
        PTi = sb("PTi", [QUADS, BLOCK])
        oT = sb("oT", [P, BLOCK])
        rec = sb("rec", [P, BLOCK])
        OT = sb("OT", [P, BLOCK])
        OUT = [sb(f"out_rows{i}", [P, BATCH, D]) for i in range(2)]

        gp = [bank(f"gates_ps{b}") for b in range(KT)]
        S = [bank(f"scores_ps{j}") for j in range(QUADS)]
        PV = bank("pv_ps")
        misc = bank("misc_ps")

        def sems(text):
            return [sem(name) for name in text.split()]

        loaded, ones_set, scaled, ready = sems("loaded ones_set weights_scaled prologue_done")
        xp_mm, xp_add, img_mm, img_copied, img_made = sems("xp_mm xp_add img_mm img_copied img_made")
        xp_split, xp_out, x_in = sems("xp_split xp_out x_in")
        xp_in = [sem(f"gate_inputs_in{i}") for i in range(2)]
        x1_evac, wst_in, x1st_in, kst_in, vst_in, k_stored, out_stored = sems(
            "x1_evac wst_in x1st_in kst_in vst_in k_stored out_stored")
        k_rounded, bst_ready, kimg_ready, vimg_ready, vimg_used = sems("k_rounded bst_ready kimg_ready vimg_ready vimg_used")
        misc_ready, misc_free = sems("misc_ready misc_free")
        p1_ready, p2_ready, exp_done = [[sem(f"{name}_{c}") for c in range(2)]
                                        for name in ("scores_ready", "scores_t_ready", "exp_done")]
        max0_done, max_done, mt_done, pv_ready, oT_ready, OT_ready = sems(
            "max0_done max_done mt_done pv_ready oT_ready OT_ready")
        g_ready, t_done, th_done, c_done, tc_done, h_done = [
            [sem(f"{name}{b}") for b in range(KT)]
            for name in ("g_ready", "t_done", "th_done", "c_done", "tc_done", "h_done")]

        block = ctx.enter_context(nc.Block())

        LOADS = [(xT, x_t), (Wx, wx), (Wh, wh), (condT, h0), (Wqk, w_qk), (Bqk, b_qk), (Wv, w_v),
                 (Bv, b_v), (Wp, w_p), (Wuk, w_uk), (Buk, b_uk), (Wuv, w_uv), (Buv, b_uv),
                 (ident, ident_in), (pickf, pick_in), (sel, sel_in), (tri, tri_in), (tri_t, tri_t_in),
                 (headc, head_col), (headr, head_row)]
        N_LOAD = 16 * (len(LOADS) + 3)

        def inner(n):
            return 0 if isinstance(n, int) else 1

        def tiles_before(ph, n):
            return BODIES * (ph - 1) + n

        def late_tiles_before(ph, n):
            return BODIES * (ph - 1 - CHUNK) + n

        def wait(eng, semaphore, count):
            if not (isinstance(count, int) and count <= 0):
                eng.wait_ge(semaphore, count)

        def misc_use(ph, n, new, old, name):
            first = not inner(n)
            names = ["xp"] * (ph < PHASES) + (["q", "k", "img1", "v"] + ["init"] * first + ["max"]) * new + ["sel"] * old + ["img2"] * new + ["proj"] * old
            before = BODIES * ph + n if ph < PHASES else BODIES * PHASES
            if ph > 0:
                before = before + 8 * tiles_before(ph, n) + (ph - 1) + inner(n) - 2 * (not (ph == 1 and first))
            return before + names.index(name)

        def wait_scores_read(eng, ph, n, j):
            if (ph if inner(n) else ph - 1) > CHUNK:
                eng.wait_ge(exp_done[1], QUADS * (late_tiles_before(ph, n) - 1) + j + 1)
            else:
                wait(eng, exp_done[0], QUADS * (tiles_before(ph, n) - 1) + j + 1)

        def chunks(blocks):
            return [(c, min(CHUNK, blocks - c)) for c in range(0, blocks, CHUNK)]

        def bodies(eng, body):
            with eng.Fori(0, BODIES) as n:
                body(0, n, 1, 0, 0)
            for ph in range(1, PHASES + 1):
                body(ph, 0, int(ph < PHASES), 1, int(ph > 1))
                with eng.Fori(1, BODIES) as n:
                    body(ph, n, int(ph < PHASES), 1, 1)
            body(PHASES + 1, 0, 0, 0, 1)

        @block.sync
        def _(sp):
            for dst, source in LOADS:
                sp.dma_start(dst[:], source).then_inc(loaded, 16)
            sp.dma_start(bx[:, :], b_x.partition_broadcast(P)).then_inc(loaded, 16)
            sp.dma_start(bp[:, :], b_p.partition_broadcast(P)).then_inc(loaded, 16)
            sp.wait_ge(ones_set, 1)
            sp.dma_start(ones_mask[1:2, :, :], mask).then_inc(loaded, 16)
            def store_gate_inputs(chunk, cols, at, pieces):
                sp.wait_ge(xp_split, 4 * pieces)
                for i in range(PARTS):
                    sp.dma_start(xp_dram[bass.ds(chunk * (P // ROWS), P // ROWS), i, :, bass.ds(cols, PIECE)],
                                 xp_parts[:, i, at:at + PIECE]).then_inc(xp_out, 16)

            def stage_gate_inputs(half, group):
                sp.dma_start(xp_st[half][0:PARTS * ROWS, :], xp_dram[group].rearrange("s r c -> (s r) c")).then_inc(xp_in[half], 16)

            def stage_x(chunk):
                sp.dma_start(x_st[:, :, :], xT[:, :, bass.ds(chunk * XCH, XCH), :].rearrange("p k t b -> p k (t b)")
                             ).then_inc(x_in, 16)

            for c in range(PIECES):
                store_gate_inputs(0, c * PIECE, c * PIECE, c + 1)
            sp.wait_ge(xp_out, 16 * PARTS * PIECES)
            sp.wait_ge(ready, 1)
            for half in range(2):
                stage_gate_inputs(half, half)
            stage_x(1)
            sp.wait_ge(loaded, N_LOAD)
            sp.dma_start(wst[:], Wqk[:, 0]).then_inc(wst_in, 16)

            def body(ph, n, lstm, new, old):
                t = BLOCK * ph + STEPS * n
                T = tiles_before(ph, n)
                cur, B = (ph - 1) % 2, ph
                if lstm:
                    group = sp.snap((2 * (BODIES * ph + n) + 2) % (2 * PHASES * BODIES))
                    chunk = sp.snap((2 * ph + 1 + n // PIECES) % (SEQ // XCH))
                    cols = sp.snap(n % PIECES * PIECE)
                    x_chunk = sp.snap((2 * ph + 1 + (n + 1) // PIECES) % (SEQ // XCH))
                batch, next_tile = (sp.snap(n // TILES), sp.snap((n + 1) % TILES)) if inner(n) else (0, 1)
                if new:
                    sp.wait_ge(x1_evac, 2 * BODIES * ph)
                    sp.dma_start(x1st[:], X1[cur][:, :, batch, :]).then_inc(x1st_in, 16)
                    if B > 1:
                        if not inner(n):
                            sp.wait_ge(k_stored, 16 * T)
                        if (B if inner(n) else B - 1) > CHUNK:
                            sp.wait_ge(p2_ready[1], QUADS * late_tiles_before(ph, n))
                        else:
                            sp.wait_ge(p2_ready[0], QUADS * T)
                        sp.dma_start(kst[:, 0:(B - 1) * BLOCK], kv_all[:, n, 0:(B - 1) * BLOCK]).then_inc(kst_in, 16)
                if lstm:
                    store_gate_inputs(chunk, cols, 0, BODIES * ph + n + PIECES + 1)
                    sp.wait_ge(misc_ready, misc_use(ph, n, new, old, "xp") + 1)
                    stage_x(x_chunk)
                if new:
                    if B < PHASES:
                        sp.wait_ge(misc_free, misc_use(ph, n, new, old, "k") + 1)
                        sp.dma_start(kv_all[:, n, (B - 1) * BLOCK:B * BLOCK],
                                     kst[:, (B - 1) * BLOCK:B * BLOCK]).then_inc(k_stored, 16)
                    sp.wait_ge(misc_ready, misc_use(ph, n, new, old, "k") + 1)
                    sp.dma_start(wst[:], Wqk[:, next_tile]).then_inc(wst_in, 16)
                if lstm:
                    sp.wait_ge(xp_out, 16 * PARTS * (BODIES * ph + n + PIECES + 1))
                    sp.wait_ge(g_ready[1], t + STEPS // 2)
                    stage_gate_inputs(0, group)
                if new:
                    sp.wait_ge(misc_free, misc_use(ph, n, new, old, "v") + 1)
                    wait(sp, pv_ready, T)
                    sp.dma_start(vst[:, 0:B, :].rearrange("p k m -> p (k m)"),
                                 kv_all[:, n, SEQ:SEQ + B * P]).then_inc(vst_in, 16)
                if lstm:
                    sp.wait_ge(g_ready[1], t + STEPS)
                    stage_gate_inputs(1, group + 1)
                if old and not inner(n):
                    i = ph - 2
                    sp.wait_ge(misc_free, misc_use(ph, n, new, old, "proj") + 1)
                    for b in range(BATCH):
                        sp.dma_start(out[b, i * BLOCK:(i + 1) * BLOCK, :], OUT[i % 2][:, b, :]).then_inc(out_stored, 16)

            bodies(sp, body)
            sp.wait_ge(out_stored, 16 * BATCH * PHASES)
            sp.wait_ge(wst_in, 16 * (BODIES * PHASES + 1))
            sp.wait_ge(xp_out, 16 * PARTS * (BODIES * PHASES + PIECES))

        @block.gpsimd
        def _(pool):
            nc.gpsimd.memset(zero[:, :], 0.0)
            nc.gpsimd.memset(ones_mask[:], 1.0).then_inc(ones_set, 1)
            pool.wait_ge(ones_set, 1)

            def split(cols, pieces, stored):
                x, parts = xps[:, cols:cols + PIECE], [xp_parts[:, i, cols:cols + PIECE] for i in range(PARTS)]
                wait(pool, xp_out, 16 * PARTS * stored)
                done = 4 * (pieces - 1)
                zeros = zero[:, :].to_broadcast([P, PIECE])
                tt = nc.gpsimd.tensor_tensor
                tt(parts[0], x, zeros, ALU.add).then_inc(xp_split, 1)
                pool.wait_ge(xp_split, done + 1)
                tt(x, x, parts[0], ALU.subtract).then_inc(xp_split, 1)
                pool.wait_ge(xp_split, done + 2)
                tt(parts[1], x, zeros, ALU.add).then_inc(xp_split, 1)
                pool.wait_ge(xp_split, done + 3)
                tt(parts[2], x, parts[1], ALU.subtract).then_inc(xp_split, 1)

            for c in range(PIECES):
                pool.wait_ge(xp_add, c + 1)
                split(c * PIECE, c + 1, 0)
            pool.wait_ge(loaded, N_LOAD)
            pool.wait_ge(img_made, 2)
            nc.gpsimd.tensor_copy(bst[:], Bqk[:, 0]).then_inc(bst_ready, 1)
            nc.gpsimd.tensor_copy(kimg_st[:], KIMG[:, 0]).then_inc(kimg_ready, 1)

            def body(ph, n, lstm, new, old):
                if lstm:
                    pool.wait_ge(misc_free, misc_use(ph, n, new, 0, "xp") + 1)
                    split(0, BODIES * ph + n + PIECES + 1, BODIES * ph + n + PIECES)
                if not new:
                    return
                if ph > 1:
                    pool.wait_ge(kst_in, 16 * (tiles_before(ph, n) - BODIES + 1))
                    old_keys = (ph - 1) * BLOCK
                    nc.gpsimd.tensor_tensor(k_r[:, 0:old_keys], kst[:, 0:old_keys],
                                            zero[:, :].to_broadcast([P, old_keys]), ALU.add).then_inc(k_rounded, 1)
                pool.wait_ge(misc_ready, misc_use(ph, n, new, old, "k") + 1)
                nc.gpsimd.tensor_copy(bst[:], Bqk[:, (n + 1) % TILES]).then_inc(bst_ready, 1)
                wait(pool, vimg_used, tiles_before(ph, n))
                nc.gpsimd.tensor_copy(vimg_st[:], VIMG[:, n]).then_inc(vimg_ready, 1)
                pool.wait_ge(misc_ready, misc_use(ph, n, new, old, "img2") + 1)
                nc.gpsimd.tensor_copy(kimg_st[:], KIMG[:, (n + 1) % BODIES]).then_inc(kimg_ready, 1)

            bodies(pool, body)

        @block.tensor
        def _(pe):
            mm = nc.tensor.matmul

            def group(b, lhsT, rhs, start, stop):
                for j in range(QUADS):
                    lo = j * D + b * HALF
                    last = mm(gp[b][LANES * j:LANES * j + BATCH, 0:HALF], lhsT, rhs[:, lo:lo + HALF],
                              start=start, stop=stop, skip_group_check=True, tile_position=(0, LANES * j))
                return last

            def inject(step):
                half, k = divmod(step, STEPS // 2)
                for b in range(KT):
                    group(b, pick[:, BATCH * k:BATCH * k + BATCH], xp_st[half], True, False)

            pe.wait_ge(scaled, 1)
            for c in range(PIECES):
                for k in range(KT):
                    last = mm(S[c][:, 0:PIECE], xT[:, k, 0:XCH, :].rearrange("p t b -> p (t b)"),
                              Wx[:, k, c * PIECE:(c + 1) * PIECE], start=k == 0, stop=k == KT - 1)
                last.then_inc(xp_mm, 1)
            pe.wait_ge(ready, 1)
            for tile in range(TILES):
                o = misc[:, BATCH * tile:BATCH * tile + BATCH]
                for k in range(KT):
                    mm(o, Wuk[:, k, tile, :], condT[:, k, :], start=k == 0, stop=False, skip_group_check=True)
                last = mm(o, Buk[:, tile, :], ones_mask[0:1, 0, 0:BATCH], start=False, stop=True, skip_group_check=True)
            last.then_inc(img_mm, 1)
            pe.wait_ge(xp_add, PIECES)
            for b in range(BATCH):
                for k in range(KT):
                    mm(S[b][0:QUADS, :], cond4[:, k, b, :], Wuv[:, k].rearrange("p t m -> p (t m)"), start=k == 0, stop=False)
                last = mm(S[b][0:QUADS, :], ones_mask[0:1, 0, 0:QUADS], Buv[:].rearrange("p t m -> p (t m)"), start=False, stop=True)
            last.then_inc(img_mm, 1)
            pe.wait_ge(img_made, 2)
            pe.wait_ge(xp_in[0], 16)
            inject(0)

            def body(ph, n, lstm, new, old):
                t = BLOCK * ph + STEPS * n
                T = tiles_before(ph, n)
                cur, B = (ph - 1) % 2, ph
                Bold = ph if inner(n) else ph - 1
                mask_at = (B - 1) * BLOCK

                def open_misc(name):
                    wait(pe, misc_free, misc_use(ph, n, new, old, name))

                def quad(j):
                    return slice(LANES * j, LANES * (j + 1))

                def scores_t(c, j, total):
                    for kb in range(c, min(c + CHUNK, total)):
                        o = S[j][:, (kb - c) * BLOCK:(kb - c + 1) * BLOCK]
                        last = mm(o, kst[quad(j), kb * BLOCK:(kb + 1) * BLOCK], qaug[quad(j), :], start=True,
                                  stop=kb != total - 1, skip_group_check=True, tile_position=(LANES * j, 0))
                        if kb == total - 1:
                            last = mm(o, identh[:, :], tri_th[:, :], start=False, stop=True, skip_group_check=True)
                    last.then_inc(p2_ready[c // CHUNK], 1)

                def values(blocks, total):
                    for kb in blocks:
                        for j in range(QUADS):
                            last = mm(PV[quad(j), 0:BLOCK], vst[:, kb, quad(j)], PT[:, j, kb, :],
                                      start=False, stop=kb == total - 1, skip_group_check=True,
                                      tile_position=(0, LANES * j))
                    return last

                for st in range(STEPS):
                    if lstm:
                        for k in range(KT):
                            pe.wait_ge(h_done[k], t + st + 1)
                            for b in range(KT):
                                last = group(b, ring[:, (st - 1) % STEPS, k, :], Wh[:, k], False, k == KT - 1)
                                if k == KT - 1:
                                    last.then_inc(g_ready[b], 1)
                    if st in (0, 1) and old and Bold > CHUNK:
                        pe.wait_ge(exp_done[0], QUADS * (T - 1) + 2 + st + 1)
                        scores_t(CHUNK, 2 + st, Bold)
                    if st in (0, 1) and lstm:
                        if st == 0:
                            open_misc("xp")
                            pe.wait_ge(x_in, 16 * (BODIES * ph + n + 1))
                        last = mm(misc[:, 0:PIECE], x_st[:, st, :], Wx[:, st, bass.ds(n % PIECES * PIECE, PIECE)],
                                  start=st == 0, stop=st == KT - 1)
                        if st == KT - 1:
                            last.then_inc(misc_ready, 1)
                    if st in (2, 3) and new:
                        which = st - 2
                        open_misc("k" if which else "q")
                        if not which:
                            pe.wait_ge(wst_in, 16 * (T + 1))
                            pe.wait_ge(bst_ready, T + 1)
                            pe.wait_ge(x1_evac, 2 * BODIES * ph)
                        for k in range(KT):
                            mm(misc[:, 0:BLOCK], wst[:, which, k, :], X1[cur][:, k, n // TILES, :], start=k == 0, stop=False)
                        mm(misc[:, 0:BLOCK], bst[:, which, :], ones_mask[:, n // TILES, mask_at:mask_at + BLOCK],
                           start=False, stop=True).then_inc(misc_ready, 1)
                    if st == 4 and new:
                        open_misc("img1")
                        pe.wait_ge(kimg_ready, T + 1)
                        mm(misc[:, 0:QUADS], qT[:, :], kimg_st[:, :], start=True, stop=True).then_inc(misc_ready, 1)
                        if B > 1:
                            pe.wait_ge(k_rounded, T - BODIES + 1)
                    if new and (st == 4 or (st == 6 and B > CHUNK)):
                        half = int(st == 6)
                        c, nb = chunks(B)[half]
                        if half:
                            pe.wait_ge(max0_done, late_tiles_before(ph, n) + 1)
                        for j in range(QUADS):
                            if not half:
                                wait_scores_read(pe, ph, n, j)
                            last = mm(S[j][:, 0:nb * BLOCK], q_r[quad(j), :], k_r[quad(j), c * BLOCK:(c + nb) * BLOCK],
                                      start=True, stop=True, tile_position=(LANES * j, 0))
                        last.then_inc(p1_ready[half], 1)
                    if st == 5 and new:
                        open_misc("v")
                        pe.wait_ge(x1st_in, 16 * (T + 1))
                        for k in range(KT):
                            mm(misc[:, 0:P], x1st[:, k, :], Wv[:, k, n % TILES, :], start=k == 0, stop=False)
                        mm(misc[:, 0:P], ones_mask[0:1, 0, 0:BLOCK], Bv[:, n % TILES, :], start=False,
                           stop=True).then_inc(misc_ready, 1)
                    if st == 6 and new and not inner(n):
                        open_misc("init")
                        for b in range(BATCH):
                            for k in range(KT):
                                lo = b * D + k * P
                                last = nc.tensor.transpose(misc[:, lo:lo + P], X1[cur][:, k, b, :], ident[:, :])
                        last.then_inc(misc_ready, 1)
                    if old and st in (7, 8, 9):
                        lo, hi = {7: (0, 2), 8: (2, 5), 9: (5, 8)}[st]
                        some = range(lo, min(hi, Bold))
                        if st == 7:
                            pe.wait_ge(vimg_ready, T)
                            mm(PV[:, 0:BLOCK], vimg_st[:, :], PTi[:, :], start=True, stop=False,
                               skip_group_check=True).then_inc(vimg_used, 1)
                            pe.wait_ge(exp_done[0], QUADS * T)
                            pe.wait_ge(vst_in, 16 * T)
                        if st == 8 and Bold > CHUNK:
                            pe.wait_ge(exp_done[1], QUADS * late_tiles_before(ph, n))
                        if some:
                            last = values(some, Bold)
                            if some[-1] == Bold - 1:
                                last.then_inc(pv_ready, 1)
                    if st == 9 and new:
                        open_misc("max")
                        pe.wait_ge(mt_done, T + 1)
                        nc.tensor.transpose(misc[:, 0:P], MT[:, :], ident[:, :]).then_inc(misc_ready, 1)
                    if new and st in (10, 11, 12, 13):
                        if st == 10:
                            pe.wait_ge(misc_free, misc_use(ph, n, new, old, "max") + 1)
                        scores_t(0, st - 10, B)
                    if st == 10 and old:
                        open_misc("sel")
                        pe.wait_ge(oT_ready, T)
                        mm(misc[:, 0:BLOCK], sel[:, :], oT[:, :], start=True, stop=True).then_inc(misc_ready, 1)
                    if st == 14 and new:
                        open_misc("img2")
                        mm(misc[0:QUADS, 0:BLOCK], kimg_st[:, :], qaug[:, :], start=True,
                           stop=True).then_inc(misc_ready, 1)
                    if new and st in (14, 15) and B > CHUNK:
                        pe.wait_ge(exp_done[0], QUADS * T + st - 14 + 1)
                        scores_t(CHUNK, st - 14, B)
                    if st == 15 and old:
                        open_misc("proj")
                        pe.wait_ge(OT_ready, T)
                        tile = (n - 1) % TILES if inner(n) else TILES - 1
                        mm(misc[:, 0:D], OT[:, :], Wp[:, tile, :], start=True, stop=True).then_inc(misc_ready, 1)
                    if lstm:
                        nxt = (st + 1) % STEPS
                        if nxt == 0:
                            pe.wait_ge(xp_in[0], 16 * (BODIES * ph + n + 2))
                        if nxt == STEPS // 2:
                            pe.wait_ge(xp_in[1], 16 * (BODIES * ph + n + 1))
                        for b in range(KT):
                            pe.wait_ge(t_done[b], t + st + 1)
                        inject(nxt)

            bodies(pe, body)

        @block.scalar
        def _(act):
            act.wait_ge(ready, 1)
            nc.scalar.activation(TC[0][:, :], condT[:, 0, :], ACT.Tanh)
            act.wait_ge(img_mm, 1)
            nc.scalar.activation(kimg[:, :].rearrange("p (b t) -> p t b", b=BATCH),
                                 misc[:, 0:BODIES].rearrange("p (t b) -> p t b", b=BATCH), ACT.Copy).then_inc(img_copied, 1)

            def body(ph, n, lstm, new, old):
                t = BLOCK * ph + STEPS * n
                T = tiles_before(ph, n)
                B = ph
                Bold = ph if inner(n) else ph - 1

                def exp(c, j, total, count):
                    nb = min(CHUNK, total - c)
                    act.wait_ge(p2_ready[c // CHUNK], count)
                    nc.scalar.activation(PT[:, j, c:c + nb, :].rearrange("p k q -> p (k q)"),
                                         S[j][:, 0:nb * BLOCK], ACT.Exp).then_inc(exp_done[c // CHUNK], 1)

                for st in range(STEPS):
                    now, nxt = st % 2, (st + 1) % 2
                    if lstm:
                        for b in range(KT):
                            act.wait_ge(t_done[b], t + st + 1)
                            nc.scalar.activation(
                                G[b][:, now, :, 0:GATES].rearrange("p r g -> p g r"),
                                Tsb[b][:, :].rearrange("p (g r) -> p g r", g=GATES)[:, :, 0:BATCH],
                                ACT.Tanh).then_inc(th_done[b], 1)
                        for b in range(KT):
                            act.wait_ge(c_done[b], t + st + 1)
                            nc.scalar.activation(TC[b][:, :], G[b][:, nxt, :, C_AT], ACT.Tanh).then_inc(tc_done[b], 1)
                    if st in (0, 1) and old and Bold > CHUNK:
                        exp(CHUNK, 2 + st, Bold, QUADS * (late_tiles_before(ph, n) - 1) + 2 + st + 1)
                    if st == 2 and new:
                        act.wait_ge(misc_ready, misc_use(ph, n, new, old, "q") + 1)
                        nc.scalar.activation(q_r[:, :], misc[:, 0:BLOCK], ACT.Copy, scale=SCALE)
                        nc.scalar.activation(qT[:, :], misc[:, 0:BLOCK], ACT.Copy, scale=SCALE).then_inc(misc_free, 1)
                    if st == 3 and new:
                        act.wait_ge(misc_ready, misc_use(ph, n, new, old, "k") + 1)
                        wait(act, k_stored, 16 * T if B < PHASES else 16 * BODIES * (PHASES - 1))
                        nc.scalar.activation(k_r[:, (B - 1) * BLOCK:B * BLOCK], misc[:, 0:BLOCK], ACT.Copy)
                        nc.scalar.activation(kst[:, (B - 1) * BLOCK:B * BLOCK], misc[:, 0:BLOCK],
                                             ACT.Copy).then_inc(misc_free, 1)
                    if st == 5 and new:
                        act.wait_ge(misc_ready, misc_use(ph, n, new, old, "v") + 1)
                        nc.scalar.activation(kv_all[:, n, SEQ + (B - 1) * P:SEQ + B * P], misc[:, 0:P], ACT.Copy).then_inc(misc_free, 1)
                    if st == 9 and old:
                        act.wait_ge(pv_ready, T)
                        nc.scalar.activation(oT[:, :], PV[:, 0:BLOCK], ACT.Copy).then_inc(oT_ready, 1)
                    if st in (10, 11, 12, 13) and new:
                        exp(0, st - 10, B, QUADS * T + st - 10 + 1)
                    if st == 14 and new:
                        act.wait_ge(misc_ready, misc_use(ph, n, new, old, "img2") + 1)
                        nc.scalar.activation(PTi[:, :], misc[0:QUADS, 0:BLOCK], ACT.Exp).then_inc(misc_free, 1)
                    if st in (14, 15) and new and B > CHUNK:
                        exp(CHUNK, st - 14, B, QUADS * late_tiles_before(ph, n) + st - 14 + 1)

            bodies(act, body)

        @block.vector
        def _(dve):
            v = nc.vector
            dve.wait_ge(loaded, N_LOAD)
            for w, of_sigmoids, of_tanh in ((Wx, 0.5, None), (Wh, 0.25, 0.5)):
                gates = w[:].rearrange("p k (m g c) -> p (k m) g c", g=GATES, c=LANES)
                v.tensor_scalar(gates[:, :, 0:3, :], gates[:, :, 0:3, :], of_sigmoids, None, ALU.mult)
                if of_tanh:
                    v.tensor_scalar(gates[:, :, 3, :], gates[:, :, 3, :], of_tanh, None, ALU.mult)
            gates = bx[:, :].rearrange("p (m g c) -> p m g c", g=GATES, c=LANES)
            v.tensor_scalar(gates[:, :, 0:3, :], gates[:, :, 0:3, :], 0.5, None, ALU.mult).then_inc(scaled, 1)
            for b in range(KT):
                v.memset(xp_st[b][:, :], 0.0)
                v.memset(gp[b][:, :], 0.0)
                v.memset(G[b][:, :, :, ONES_AT:ONES_AT + 2], 1.0)
                v.memset(G[b][:, 0, :, C_AT:C_AT + 1], 0.0)
            v.memset(MT[:, :], 0.0)
            v.tensor_copy(identh[:, :], ident[:, :])
            v.tensor_copy(tri_th[:, :], tri_t[:, :])
            v.tensor_copy(pick[:, :], pickf[:, :])
            for r in range(QUADS):
                v.tensor_copy(cond4[:, :, :, r], condT[:, :, :])
            for k in range(KT):
                v.tensor_scalar(ring[:, STEPS - 1, k, :], condT[:, k, :], 2.0, None, ALU.mult).then_inc(h_done[k], 1)
            v.memset(products[0][:, :, :], 0.0).then_inc(ready, 1)
            dve.wait_ge(scaled, 1)
            for c in range(PIECES):
                dve.wait_ge(xp_mm, c + 1)
                cols = slice(c * PIECE, (c + 1) * PIECE)
                v.tensor_tensor(xps[:, cols], S[c][:, 0:PIECE], bx[:, cols], ALU.add).then_inc(xp_add, 1)
            dve.wait_ge(img_copied, 1)
            v.tensor_tensor(KIMG[:, :, :], kimg[:, :].unsqueeze(2).to_broadcast([P, BODIES, QUADS]),
                            headc[:, :].unsqueeze(1).to_broadcast([P, BODIES, QUADS]), ALU.mult).then_inc(img_made, 1)
            dve.wait_ge(img_mm, 2)
            for b in range(BATCH):
                last = v.tensor_tensor(VIMG[:, b * TILES:(b + 1) * TILES, :],
                                       S[b][0:QUADS, :].rearrange("p (t m) -> p t m", t=TILES),
                                       headr[:, :].unsqueeze(1).to_broadcast([QUADS, TILES, P]), ALU.mult)
            last.then_inc(img_made, 1)

            def body(ph, n, lstm, new, old):
                t = BLOCK * ph + STEPS * n
                T = tiles_before(ph, n)
                cols = dve.snap(n % PIECES * PIECE) if lstm else None
                cur, B = (ph - 1) % 2, ph

                def maxima(c, j):
                    full = min(CHUNK, B - 1 - c)
                    if full > 0:
                        last = v.reduce_max(mx[:, j, 2 + c // CHUNK:3 + c // CHUNK], S[j][:, 0:full * BLOCK], AX)
                    if full < CHUNK:
                        last = v.tensor_tensor_reduce(out=junk[:, j, :], in0=S[j][:, full * BLOCK:(full + 1) * BLOCK],
                                                      in1=tri[:, :], scale=1.0, scalar=NEG, op0=ALU.add, op1=ALU.max,
                                                      accum_out=mx[:, j, 1:2])
                    return last

                for st in range(STEPS):
                    now, nxt = st % 2, (st + 1) % 2
                    if lstm:
                        for b in range(KT):
                            dve.wait_ge(g_ready[b], t + st + 1)
                            v.transpose(Tsb[b][:, :], gp[b][:, 0:HALF]).then_inc(t_done[b], 1)
                        for b in range(KT):
                            dve.wait_ge(th_done[b], t + st + 1)
                            for r in range(BATCH):
                                last = v.tensor_tensor_reduce(
                                    out=products[b][:, r, :].rearrange("p (a k) -> p a k", a=2),
                                    in0=G[b][:, now, r, :].rearrange("p (a k) -> p a k", a=2)[:, :, 0:2],
                                    in1=G[b][:, now, r, GATES - 1:C_AT + 1:C_AT - GATES + 1].unsqueeze(1).to_broadcast([P, 2, 2]),
                                    scale=0.5, scalar=0.0, op0=ALU.mult, op1=ALU.add,
                                    accum_out=G[b][:, nxt, r, C_AT:C_AT + 1])
                            last.then_inc(c_done[b], 1)
                        for b in range(KT):
                            dve.wait_ge(tc_done[b], t + st + 1)
                            v.scalar_tensor_tensor(ring[:, st, b, :], G[b][:, now, :, 2], 1.0, TC[b][:, :],
                                                   ALU.add, ALU.mult).then_inc(h_done[b], 1)
                    if st == 1 and lstm:
                        dve.wait_ge(misc_ready, misc_use(ph, n, new, old, "xp") + 1)
                        dve.wait_ge(xp_split, 4 * (BODIES * ph + n + PIECES))
                        v.tensor_tensor(xps[:, 0:PIECE], misc[:, 0:PIECE], bx[:, bass.ds(cols, PIECE)],
                                        ALU.add).then_inc(misc_free, 1)
                    if st == 4 and new:
                        dve.wait_ge(p1_ready[0], T + 1)
                        dve.wait_ge(misc_ready, misc_use(ph, n, new, old, "img1") + 1)
                        v.tensor_copy(mx[:, :, 0], misc[:, 0:QUADS]).then_inc(misc_free, 1)
                    if st in (4, 5) and new:
                        for j in (0, 1) if st == 4 else (2, 3):
                            last = maxima(0, j)
                        if st == 5 and B > CHUNK:
                            last.then_inc(max0_done, 1)
                        elif st == 5:
                            last.then_inc(max_done, 1)
                    if st in (6, 7) and new and B > CHUNK:
                        if st == 6:
                            dve.wait_ge(p1_ready[1], late_tiles_before(ph, n) + 1)
                            if B == CHUNK + 1:
                                v.tensor_copy(mx[:, :, 3], mx[:, :, 0])
                        for j in (0, 1) if st == 6 else (2, 3):
                            last = maxima(CHUNK, j)
                        if st == 7:
                            last.then_inc(max_done, 1)
                    if st == 6 and new and not inner(n):
                        dve.wait_ge(misc_ready, misc_use(ph, n, new, old, "init") + 1)
                        wait(dve, out_stored, 16 * BATCH * (ph - 2))
                        v.tensor_tensor(OUT[cur][:, :, :], misc[:, :].rearrange("p (b f) -> p b f", b=BATCH),
                                        bp[:, :].unsqueeze(1).to_broadcast([P, BATCH, D]), ALU.add).then_inc(misc_free, 1)
                    if lstm and st in (7, 15):
                        half = int(st == 15)
                        at = t + half * STEPS // 2
                        where = STEPS * n + half * STEPS // 2
                        for k in range(KT):
                            dve.wait_ge(h_done[k], at + STEPS // 2 + 1)
                        for b in range(BATCH):
                            last = v.scalar_tensor_tensor(
                                X1[ph % 2][:, :, b, bass.ds(where, STEPS // 2)],
                                ring[:, half * STEPS // 2:(half + 1) * STEPS // 2, :, b].rearrange("p t k -> p k t"), 0.5,
                                xT[:, :, bass.ds(at, STEPS // 2), b], ALU.mult, ALU.add)
                        last.then_inc(x1_evac, 1)
                    if st == 8 and new:
                        dve.wait_ge(max_done, T + 1)
                        parts = 2 + (B > 1) + (B > CHUNK + 1)
                        v.tensor_reduce(MT[:, MAX_ROW::LANES], mx[:, :, 0:parts], AX, ALU.max,
                                        negate=True).then_inc(mt_done, 1)
                    if st == 9 and new:
                        dve.wait_ge(misc_ready, misc_use(ph, n, new, old, "max") + 1)
                        v.tensor_tensor(qaug[:, :], qT[:, :], misc[:, 0:BLOCK], ALU.add).then_inc(misc_free, 1)
                    if st == 10 and old:
                        dve.wait_ge(misc_ready, misc_use(ph, n, new, old, "sel") + 1)
                        v.reciprocal(rec[:, 0:BLOCK // 2], misc[:, 0:BLOCK // 2])
                    if st == 11 and old:
                        v.reciprocal(rec[:, BLOCK // 2:], misc[:, BLOCK // 2:BLOCK]).then_inc(misc_free, 1)
                    if st == 12 and old:
                        dve.wait_ge(misc_free, misc_use(ph, n, new, old, "sel") + 1)
                        v.tensor_tensor(OT[:, :], oT[:, :], rec[:, :], ALU.mult).then_inc(OT_ready, 1)
                    if st == 15 and old:
                        o = OUT[cur][:, (n - 1) // TILES, :] if inner(n) else OUT[1 - cur][:, BATCH - 1, :]
                        dve.wait_ge(misc_ready, misc_use(ph, n, new, old, "proj") + 1)
                        v.tensor_tensor(o, o, misc[:, 0:D], ALU.add).then_inc(misc_free, 1)

            bodies(dve, body)


def _positions():
    import numpy as np
    feature = np.array([[64 * (q // 32) + 32 * k + q % 32 for q in range(128)] for k in range(2)])
    column = np.array([256 * g + 64 * j + 32 * b + p for j in range(4) for b in range(2) for g in range(4) for p in range(32)])
    return feature, column


def kernel(**inputs):
    import numpy as np
    import concourse.bacc as _bacc
    from concourse import mybir as _mybir
    from concourse.bass_utils import run_bass_kernel_spmd as _run

    g = {k: np.asarray(v) for k, v in inputs.items()}
    feature, column = _positions()

    def by_feature(w):
        return w[feature].transpose(1, 0, *range(2, w.ndim + 1))

    def in_slots(w, ones=()):
        w = w.reshape(*w.shape[:-1], TILES, QUADS, HDIM)
        padded = np.zeros((*w.shape[:-1], LANES), np.float32)
        padded[..., :HDIM] = w
        for at, value in ones:
            padded[..., at] = value
        return padded.reshape(*w.shape[:-3], TILES, P)

    c_w, c_b = g["L1_cond_c_attn_w"], g["L1_cond_c_attn_b"]
    w_qk = np.stack([in_slots(by_feature(c_w[:, i * D:(i + 1) * D])) for i in range(2)], 1)
    b_q = in_slots(c_b[0:D], [(MASK_ROW, 1 / SCALE)])
    b_k = in_slots(c_b[D:2 * D], [(MAX_ROW, 1.0)])
    mask_slot = in_slots(np.zeros(D, np.float32), [(MASK_ROW, 1.0)])
    b_qk = np.stack([np.stack([b_q, b_k], 1), np.stack([np.zeros_like(b_q), mask_slot], 1)])
    rows = in_slots(np.ascontiguousarray(g["L1_cond_c_proj_w"].T)).transpose(2, 1, 0)
    block = np.arange(P) // LANES
    arrays = {
        "x_t": by_feature(g["x"].transpose(2, 1, 0)),
        "wx": by_feature(g["L0_cond_Wx"][:, column]),
        "wh": by_feature(g["L0_cond_Wh"][:, column]),
        "b_x": g["L0_cond_b"][column],
        "h0": by_feature(g["cond_1024"].T),
        "w_qk": w_qk.transpose(0, 3, 1, 2, 4),
        "b_qk": b_qk,
        "w_v": in_slots(by_feature(c_w[:, 2 * D:])),
        "b_v": in_slots(c_b[2 * D:], [(HDIM, 1.0)])[None],
        "w_p": rows[:, :, feature.reshape(-1)],
        "b_p": g["L1_cond_c_proj_b"][feature.reshape(-1)],
        "w_uk": in_slots(by_feature(g["L1_cond_uk_w"].T)),
        "b_uk": in_slots(g["L1_cond_uk_b"], [(MAX_ROW, 1.0)])[None],
        "w_uv": in_slots(by_feature(g["L1_cond_uv_w"].T)),
        "b_uv": in_slots(g["L1_cond_uv_b"], [(HDIM, 1.0)])[None],
        "mask": g["mask_Bx1x1xS_ff0"].reshape(1, BATCH, SEQ),
        "ident_in": np.eye(P, dtype=np.float32),
        "pick_in": ((np.arange(P)[:, None] % ROWS == np.arange(ROWS)) & (np.arange(P)[:, None] < PARTS * ROWS)).astype(np.float32),
        "sel_in": ((np.arange(P)[:, None] % LANES == HDIM) & (block[:, None] == block)).astype(np.float32),
        "tri_in": np.where(np.arange(P)[None] > np.arange(P)[:, None], np.float32(NEG), np.float32(0)),
        "tri_t_in": np.where(np.arange(P)[:, None] > np.arange(P)[None], np.float32(NEG), np.float32(0)),
        "head_col": (block[:, None] == np.arange(QUADS)).astype(np.float32),
        "head_row": (np.arange(QUADS)[:, None] == block).astype(np.float32),
    }
    arrays = {k: np.ascontiguousarray(v) for k, v in arrays.items()}
    nc = _bacc.Bacc("TRN2", target_bir_lowering=False, num_devices=1)
    args = {k: nc.dram_tensor(k, v.shape, _mybir.dt.float32, kind="ExternalInput").ap() for k, v in arrays.items()}
    out = nc.dram_tensor("out", (BATCH, SEQ, D), _mybir.dt.float32, kind="ExternalOutput").ap()
    lstm_attention(nc, **args, out=out)
    r = _run(nc, [arrays], core_ids=[0])
    rows = r.results[0]["out"]
    return rows.reshape(BATCH, SEQ, KT, QUADS, LANES).transpose(0, 1, 3, 2, 4).reshape(BATCH, SEQ, D)
```

```python
from contextlib import ExitStack

import concourse.bass as bass
from concourse import mybir

F32 = mybir.dt.float32
F32R = mybir.dt.float32r
BF16 = mybir.dt.bfloat16
ALU = mybir.AluOpType
ACT = mybir.ActivationFunctionType
AX = mybir.AxisListType.X

P = 128
BATCH, SEQ, D = 2, 1024, 256
HEADS, HDIM = 16, 16
KT = D // P
QUADS = 4
LANES = 32
GATES = 4
HALF = GATES * LANES
STEPS = 16
BLOCK = P
PHASES = SEQ // BLOCK
BODIES = BLOCK // STEPS
TILES = HEADS // QUADS
ROWS = STEPS // 2 * BATCH
PARTS = 3
CHUNK = 4
XCH = P // BATCH
PIECE = 256
PIECES = GATES * D // PIECE
CHUNKS = SEQ // XCH
MASK_ROW, MAX_ROW = HDIM, HDIM + 1
NEG = -1e30
G_AT, O_AT, ONES_AT, C_AT = 2, 3, 4, 6
SCALE = HDIM ** -0.5


def lstm_attention(nc, x_t, wx, wh, b_x, h0, w_qk, b_qk, w_v, b_v, w_p, b_p, w_uk, b_uk, w_uv, b_uv,
                   mask, ident_in, pick_in, sel_in, tri_in, tri_t_in, head_col, out):
    ctx = ExitStack()
    with ctx:
        def sb(name, shape, dt=F32):
            return ctx.enter_context(nc.sbuf_tensor(name, shape, dt))

        def bank(name):
            return ctx.enter_context(nc.psum_tensor(name, [P, 512], F32))

        def sem(name):
            return ctx.enter_context(nc.semaphore(name))

        xp_dram = nc.dram_tensor("gate_inputs", (SEQ * BATCH // ROWS, PARTS, ROWS, GATES * D), BF16,
                                 kind="Internal").ap()

        xT = sb("xT", [P, KT, SEQ, BATCH])
        Wx = sb("Wx", [P, KT, GATES * D])
        Wh = sb("Wh", [P, KT, GATES * D])
        bx = sb("bx", [P, GATES * D])
        condT = sb("condT", [P, KT, BATCH])
        Wqk = sb("Wqk", [P, TILES, 2, KT, P])
        Bqk = sb("Bqk", [2, TILES, 2, P])
        Wv = sb("Wv", [P, KT, TILES, P])
        Bv = sb("Bv", [1, TILES, P])
        Wp = sb("Wp", [P, TILES, D])
        bp = sb("bp", [P, D])
        Buk = sb("Buk", [1, TILES, P])
        Buv = sb("Buv", [1, TILES, P])
        ones_mask = sb("ones_mask", [2, BATCH, SEQ])
        ident = sb("ident", [P, P])
        identh = sb("identh", [P, P], BF16)
        sel = sb("sel", [P, P])
        tri = sb("tri", [P, P])
        tri_t = sb("tri_t", [P, P])
        tri_h = sb("tri_h", [P, P], BF16)
        tri_th = sb("tri_th", [P, P], BF16)
        headc = sb("headc", [P, QUADS])
        xp_st = [sb(f"xp_st{i}", [P, GATES * D], BF16) for i in range(2)]
        pick = sb("pick_rows", [P, ROWS], BF16)
        pickf = sb("pick_rows_f32", [P, ROWS])
        zero = sb("zero", [P, 1])
        x_st = sb("x_st", [P, 2, KT, XCH * BATCH])
        Tsb = [sb(f"gates_t{b}", [P, HALF]) for b in range(KT)]
        G = [sb(f"gates{b}", [P, 2, BATCH, 8]) for b in range(KT)]
        products = [sb(f"products{b}", [P, BATCH, 4]) for b in range(KT)]
        TC = [sb(f"tanh_c{b}", [P, BATCH]) for b in range(KT)]
        ring = sb("h2_ring", [P, STEPS, KT, BATCH])
        X1 = [sb(f"x1_{i}", [P, KT, BATCH, BLOCK]) for i in range(2)]
        xp_parts = sb("xp_parts", [P, PARTS, GATES * D], BF16)
        kv_all = sb("kv_all", [P, BODIES, SEQ + PHASES * P])
        KIMG = sb("KIMG", [P, BODIES, QUADS])
        img = sb("img", [P, 2, BODIES])
        VIMG_T = sb("VIMG_T", [P, BODIES, QUADS])
        VIMG = sb("VIMG", [QUADS, BODIES, P])
        wst = sb("wst", [P, 2, KT, P])
        bst = sb("bst", [2, 2, P])
        x1st = sb("x1st", [P, KT, BLOCK])
        kst = sb("kst", [P, SEQ])
        vst = sb("vst", [P, PHASES, P])
        Wuk = kst[:, :].rearrange("p (k t m) -> p k t m", k=KT, t=TILES)
        Wuv = vst[:, :, :].rearrange("p (k t) m -> p k t m", k=KT)
        kimg_st = sb("kimg_st", [P, QUADS])
        vimg_st = sb("vimg_st", [QUADS, P])
        qT = sb("qT", [P, BLOCK])
        q_r = sb("q_rounded", [P, BLOCK], F32R)
        k_r = sb("k_rounded", [P, SEQ], F32R)
        q_head = sb("q_head", [P, QUADS, BLOCK])
        mx = sb("mx", [P, QUADS, 3])
        MT = sb("MT", [P, P])
        PT = sb("PT", [P, QUADS, PHASES, BLOCK])
        xps = PT[:, 0, :, :].rearrange("p k q -> p (k q)")
        PTi = sb("PTi", [QUADS, BLOCK])
        oT = sb("oT", [P, BLOCK])
        rec = sb("rec", [P, BLOCK])
        OT = sb("OT", [P, BLOCK])
        OUT = [sb(f"out_rows{i}", [P, BATCH, D]) for i in range(2)]

        gp = [bank(f"gates_ps{b}") for b in range(KT)]
        S = [bank(f"scores_ps{j}") for j in range(QUADS)]
        PV = bank("pv_ps")
        misc = bank("misc_ps")

        def sems(text):
            return [sem(name) for name in text.split()]

        loaded_first, loaded, ones_set, scaled, ready = sems("loaded_first loaded ones_set weights_scaled prologue_done")
        xp_mm, xp_add, img_mm, img_copied, img_made, masks_made = sems("xp_mm xp_add img_mm img_copied img_made masks_made")
        kst_half_in = [sem(f"kst_half_in{c}") for c in range(2)]
        xp_split, xp_out = sems("xp_split xp_out")
        x_in = [sem(f"x_in{u}") for u in range(2)]
        xp_in = [sem(f"gate_inputs_in{i}") for i in range(2)]
        x1_evac, wst_in, x1st_in, kst_in, vst_in, k_stored, out_stored = sems(
            "x1_evac wst_in x1st_in kst_in vst_in k_stored out_stored")
        last_scores, last_max, k_rounded, bst_ready, kimg_ready, vimg_ready, vimg_used = sems("last_scores last_max k_rounded bst_ready kimg_ready vimg_ready vimg_used")
        misc_ready, misc_free = sems("misc_ready misc_free")
        p1_ready, p2_ready, exp_done = [[sem(f"{name}_{c}") for c in range(2)]
                                        for name in ("scores_ready", "scores_t_ready", "exp_done")]
        max0_done, max_done, mt_done, pv_ready, oT_ready, OT_ready = sems(
            "max0_done max_done mt_done pv_ready oT_ready OT_ready")
        g_ready, ifg_done, t_done, th_done, tho_done, c_done, tc_done, h_done = [
            [sem(f"{name}{b}") for b in range(KT)]
            for name in ("g_ready", "ifg_done", "t_done", "th_done", "tho_done", "c_done", "tc_done", "h_done")]

        block = ctx.enter_context(nc.Block())

        FIRST_X = 3 * XCH
        FIRST = [(Wx[:], wx), (xT[:, :, 0:FIRST_X, :], x_t[:, :, 0:FIRST_X, :]), (bx[:, :], b_x.partition_broadcast(P)),
                 (condT[:], h0), (pickf[:], pick_in), (Wh[:], wh)]
        REST = [(xT[:, :, FIRST_X:, :], x_t[:, :, FIRST_X:, :]), (ident[:], ident_in), (sel[:], sel_in),
                (tri[:], tri_in), (tri_t[:], tri_t_in), (headc[:], head_col), (Wqk[:], w_qk), (Bqk[:], b_qk),
                (Wv[:], w_v), (Bv[:], b_v), (Wp[:], w_p), (Wuk, w_uk), (Buk[:], b_uk), (Wuv, w_uv), (Buv[:], b_uv),
                (bp[:, :], b_p.partition_broadcast(P)), (ones_mask[1:2, :, :], mask)]

        def inner(n):
            return 0 if isinstance(n, int) else 1

        def tiles_before(ph, n):
            return BODIES * (ph - 1) + n

        def late_tiles_before(ph, n):
            return BODIES * (ph - 1 - CHUNK) + n

        def wait(eng, semaphore, count):
            if not (isinstance(count, int) and count <= 0):
                eng.wait_ge(semaphore, count)

        def misc_use(ph, n, new, old, name):
            first = not inner(n)
            names = (["q", "k", "img1", "v"] + ["init"] * first + ["max"]) * new + ["sel", "proj"] * old + ["img2"] * new
            before = 8 * tiles_before(ph, n) + (ph - 1) + inner(n) - 2 * (not (ph == 1 and first))
            return before + names.index(name)

        def wait_scores_read(eng, ph, n, j):
            if (ph if inner(n) else ph - 1) > CHUNK:
                eng.wait_ge(exp_done[1], QUADS * (late_tiles_before(ph, n) - 1) + j + 1)
            else:
                wait(eng, exp_done[0], QUADS * (tiles_before(ph, n) - 1) + j + 1)

        def chunks(blocks):
            return [(c, min(CHUNK, blocks - c)) for c in range(0, blocks, CHUNK)]

        def bodies(eng, body):
            with eng.Fori(0, BODIES) as n:
                body(0, n, 1, 0, 0)
            for ph in range(1, PHASES):
                body(ph, 0, 1, 1, int(ph > 1))
                with eng.Fori(1, BODIES) as n:
                    body(ph, n, 1, 1, 1)
            body(PHASES, 0, 0, 0, 1)

        BEFORE = BODIES * (PHASES - 1)
        USES_BEFORE = 8 * BEFORE + PHASES - 1

        def lead(n):
            return isinstance(n, int) and n < 0

        def last_use(n, name):
            if lead(n):
                return USES_BEFORE + ["q", "k", "img1", "v", "init", "max"].index(name)
            first, end = isinstance(n, int) and n == 0, isinstance(n, int) and n == BODIES - 1
            names = (["img2"] + ["q"] * (not end) + ["proj"] * (not first) + ["k", "img1", "v", "max"] * (not end)
                     + ["sel"] + ["end"] * end)
            return USES_BEFORE + 6 + (0 if first else 8 * n - 1) + names.index(name)

        def last_bodies(eng, body):
            body(-1, 1, 0)
            body(0, 1, 0)
            with eng.Fori(1, BODIES - 1) as n:
                body(n, 1, 1)
            body(BODIES - 1, 0, 1)

        @block.sync
        def _(sp):
            for dst, source in FIRST:
                sp.dma_start(dst, source).then_inc(loaded_first, 16)
            sp.wait_ge(ones_set, 1)
            for dst, source in REST:
                sp.dma_start(dst, source).then_inc(loaded, 16)

            def store_gate_inputs(chunk, chunks):
                sp.wait_ge(xp_split, 4 * PIECES * chunks)
                for i in range(PARTS):
                    sp.dma_start(xp_dram[bass.ds(chunk * (P // ROWS), P // ROWS), i, :, :],
                                 xp_parts[:, i, :]).then_inc(xp_out, 16)

            def stage_gate_inputs(half, group):
                sp.dma_start(xp_st[half][0:PARTS * ROWS, :],
                             xp_dram[group].rearrange("s r c -> (s r) c")).then_inc(xp_in[half], 16)

            def stage_x(u, chunk):
                sp.dma_start(x_st[:, u, :, :], xT[:, :, bass.ds(chunk * XCH, XCH), :].rearrange("p k t b -> p k (t b)")
                             ).then_inc(x_in[u], 16)

            sp.wait_ge(loaded_first, 16 * len(FIRST))
            for u in range(2):
                stage_x(u, 1 + u)
            store_gate_inputs(0, 1)
            sp.wait_ge(xp_out, 16 * PARTS)
            sp.wait_ge(ready, 1)
            for half in range(2):
                stage_gate_inputs(half, half)
            sp.wait_ge(loaded, 16 * len(REST))
            sp.dma_start(wst[:], Wqk[:, 0]).then_inc(wst_in, 16)

            def body(ph, n, lstm, new, old):
                t = BLOCK * ph + STEPS * n
                T = tiles_before(ph, n)
                cur, B = (ph - 1) % 2, ph
                if lstm:
                    group = sp.snap((2 * (BODIES * ph + n) + 2) % (2 * PHASES * BODIES))
                if ph == 0:
                    chunk = [sp.snap((2 * n + 1 + u) % CHUNKS) for u in range(2)]
                    next_chunk = [sp.snap((2 * n + 3 + u) % CHUNKS) for u in range(2)]
                batch, next_tile = (sp.snap(n // TILES), sp.snap((n + 1) % TILES)) if inner(n) else (0, 1)
                if new:
                    sp.wait_ge(x1_evac, 2 * BODIES * ph)
                    sp.dma_start(x1st[:], X1[cur][:, :, batch, :]).then_inc(x1st_in, 16)
                    if B > 1:
                        if not inner(n):
                            sp.wait_ge(k_stored, 16 * T)
                        if (B if inner(n) else B - 1) > CHUNK:
                            sp.wait_ge(p2_ready[1], QUADS * late_tiles_before(ph, n))
                        else:
                            sp.wait_ge(p2_ready[0], QUADS * T)
                        sp.dma_start(kst[:, 0:(B - 1) * BLOCK], kv_all[:, n, 0:(B - 1) * BLOCK]).then_inc(kst_in, 16)
                if ph == 0:
                    sp.wait_ge(xp_mm, PIECES * (2 * n + 2))
                    stage_x(0, next_chunk[0])
                    store_gate_inputs(chunk[0], 2 * n + 2)
                if new:
                    if B < PHASES:
                        sp.wait_ge(misc_free, misc_use(ph, n, new, old, "k") + 1)
                        sp.dma_start(kv_all[:, n, (B - 1) * BLOCK:B * BLOCK],
                                     kst[:, (B - 1) * BLOCK:B * BLOCK]).then_inc(k_stored, 16)
                    sp.wait_ge(misc_ready, misc_use(ph, n, new, old, "k") + 1)
                    sp.dma_start(wst[:], Wqk[:, next_tile]).then_inc(wst_in, 16)
                if lstm:
                    sp.wait_ge(xp_out, 16 * PARTS * (2 * n + 1 if ph == 0 else CHUNKS + 1))
                    sp.wait_ge(g_ready[1], t + STEPS // 2)
                    stage_gate_inputs(0, group)
                if new:
                    sp.wait_ge(misc_free, misc_use(ph, n, new, old, "v") + 1)
                    wait(sp, pv_ready, T)
                    sp.dma_start(vst[:, 0:B, :].rearrange("p k m -> p (k m)"),
                                 kv_all[:, n, SEQ:SEQ + B * P]).then_inc(vst_in, 16)
                if lstm:
                    sp.wait_ge(g_ready[1], t + STEPS)
                    stage_gate_inputs(1, group + 1)
                if ph == 0:
                    sp.wait_ge(xp_mm, PIECES * (2 * n + 3))
                    stage_x(1, next_chunk[1])
                    store_gate_inputs(chunk[1], 2 * n + 3)
                if old and not inner(n):
                    i = ph - 2
                    sp.wait_ge(misc_free, misc_use(ph, n, new, old, "proj") + 1)
                    for b in range(BATCH):
                        sp.dma_start(out[b, i * BLOCK:(i + 1) * BLOCK, :], OUT[i % 2][:, b, :]).then_inc(out_stored, 16)

            bodies(sp, body)

            def last_body(n, start, before):
                if not start:
                    return
                m, T = n + 1, BEFORE + n + 1
                batch, tile, next_tile = ((m // TILES, m % TILES, (m + 1) % TILES) if isinstance(n, int) else
                                          (sp.snap(m // TILES), sp.snap(m % TILES), sp.snap((m + 1) % TILES)))
                sp.wait_ge(x1_evac, 2 * BODIES * PHASES)
                sp.dma_start(x1st[:], X1[(PHASES - 1) % 2][:, :, batch, :]).then_inc(x1st_in, 16)
                sp.wait_ge(misc_ready, last_use(n, "k") + 1)
                sp.dma_start(wst[:], Wqk[:, next_tile]).then_inc(wst_in, 16)
                sp.wait_ge(k_stored, 16 * BEFORE)
                sp.wait_ge(p2_ready[0], QUADS * T)
                sp.dma_start(kst[:, 0:SEQ // 2], kv_all[:, m, 0:SEQ // 2]).then_inc(kst_half_in[0], 16)
                sp.wait_ge(misc_free, last_use(n, "k") + 1)
                sp.wait_ge(p2_ready[1], QUADS * (T - BODIES * CHUNK))
                sp.dma_start(kst[:, SEQ // 2:], kv_all[:, m, SEQ // 2:SEQ]).then_inc(kst_half_in[1], 16)
                sp.wait_ge(misc_free, last_use(n, "v") + 1)
                sp.wait_ge(pv_ready, T)
                sp.dma_start(vst[:, :, :].rearrange("p k m -> p (k m)"), kv_all[:, m, SEQ:]).then_inc(vst_in, 16)

            last_bodies(sp, last_body)
            sp.wait_ge(misc_free, last_use(BODIES - 1, "end") + 1)
            for b in range(BATCH):
                sp.dma_start(out[b, SEQ - BLOCK:, :], OUT[(PHASES - 1) % 2][:, b, :]).then_inc(out_stored, 16)
            sp.wait_ge(out_stored, 16 * BATCH * PHASES)
            sp.wait_ge(wst_in, 16 * (BODIES * PHASES + 1))
            sp.wait_ge(xp_out, 16 * PARTS * (CHUNKS + 1))
            for u in range(2):
                sp.wait_ge(x_in[u], 16 * (BODIES + 1))

        @block.gpsimd
        def _(pool):
            nc.gpsimd.memset(zero[:, :], 0.0)
            nc.gpsimd.memset(ones_mask[:], 1.0).then_inc(ones_set, 1)
            pool.wait_ge(ones_set, 1)

            def split(piece, pieces, chunks):
                cols = slice(piece * PIECE, (piece + 1) * PIECE)
                x, parts = xps[:, cols], [xp_parts[:, i, cols] for i in range(PARTS)]
                pool.wait_ge(xp_add, pieces)
                wait(pool, xp_out, 16 * PARTS * chunks)
                done = 4 * (pieces - 1)
                zeros = zero[:, :].to_broadcast([P, PIECE])
                tt = nc.gpsimd.tensor_tensor
                tt(parts[0], x, zeros, ALU.add).then_inc(xp_split, 1)
                pool.wait_ge(xp_split, done + 1)
                tt(x, x, parts[0], ALU.subtract).then_inc(xp_split, 1)
                pool.wait_ge(xp_split, done + 2)
                tt(parts[1], x, zeros, ALU.add).then_inc(xp_split, 1)
                pool.wait_ge(xp_split, done + 3)
                tt(parts[2], x, parts[1], ALU.subtract).then_inc(xp_split, 1)

            for c in range(PIECES):
                split(c, c + 1, 0)
            pool.wait_ge(loaded, 16 * len(REST))
            nc.gpsimd.tensor_copy(bst[:], Bqk[:, 0]).then_inc(bst_ready, 1)

            def body(ph, n, lstm, new, old):
                if ph == 0:
                    for i in range(2 * PIECES):
                        split(i % PIECES, PIECES * (2 * n + 1) + i + 1, 2 * n + 1 + i // PIECES)
                if not new:
                    return
                first = ph == 1 and not inner(n)
                if first:
                    pool.wait_ge(img_made, 1)
                    nc.gpsimd.tensor_copy(kimg_st[:], KIMG[:, 0]).then_inc(kimg_ready, 1)
                if ph > 1:
                    pool.wait_ge(kst_in, 16 * (tiles_before(ph, n) - BODIES + 1))
                    old_keys = (ph - 1) * BLOCK
                    nc.gpsimd.tensor_tensor(k_r[:, 0:old_keys], kst[:, 0:old_keys],
                                            zero[:, :].to_broadcast([P, old_keys]), ALU.add).then_inc(k_rounded, 1)
                pool.wait_ge(misc_ready, misc_use(ph, n, new, old, "k") + 1)
                nc.gpsimd.tensor_copy(bst[:], Bqk[:, (n + 1) % TILES]).then_inc(bst_ready, 1)
                wait(pool, vimg_used, tiles_before(ph, n))
                if first:
                    pool.wait_ge(img_made, 3)
                nc.gpsimd.tensor_copy(vimg_st[:], VIMG[:, n]).then_inc(vimg_ready, 1)
                pool.wait_ge(misc_ready, misc_use(ph, n, new, old, "img2") + 1)
                nc.gpsimd.tensor_copy(kimg_st[:], KIMG[:, (n + 1) % BODIES]).then_inc(kimg_ready, 1)

            bodies(pool, body)

            def last_body(n, start, before):
                if not start:
                    return
                m, T = n + 1, BEFORE + n + 1
                pool.wait_ge(k_stored, 16 * BEFORE)
                if lead(n):
                    pool.wait_ge(p1_ready[1], QUADS * (BEFORE - BODIES * CHUNK))
                else:
                    pool.wait_ge(last_scores, 2 * QUADS * m)
                old_keys = SEQ - BLOCK
                nc.gpsimd.tensor_tensor(k_r[:, 0:old_keys], kv_all[:, m, 0:old_keys],
                                        zero[:, :].to_broadcast([P, old_keys]), ALU.add).then_inc(k_rounded, 1)
                if not lead(n):
                    pool.wait_ge(misc_ready, last_use(n, "img2") + 1)
                    nc.gpsimd.tensor_copy(kimg_st[:], KIMG[:, m]).then_inc(kimg_ready, 1)
                pool.wait_ge(misc_ready, last_use(n, "k") + 1)
                nc.gpsimd.tensor_copy(bst[:], Bqk[:, (m + 1) % TILES]).then_inc(bst_ready, 1)
                pool.wait_ge(vimg_used, T)
                nc.gpsimd.tensor_copy(vimg_st[:], VIMG[:, m]).then_inc(vimg_ready, 1)

            last_bodies(pool, last_body)

        @block.tensor
        def _(pe):
            mm = nc.tensor.matmul

            def group(b, lhsT, rhs, start, stop):
                for j in range(QUADS):
                    lo = j * D + b * HALF
                    last = mm(gp[b][LANES * j:LANES * j + BATCH, 0:HALF], lhsT, rhs[:, lo:lo + HALF],
                              start=start, stop=stop, skip_group_check=True, tile_position=(0, LANES * j))
                return last

            def inject(step):
                half, k = divmod(step, STEPS // 2)
                for b in range(KT):
                    group(b, pick[:, BATCH * k:BATCH * k + BATCH], xp_st[half], True, False)

            pe.wait_ge(scaled, 1)
            for c in range(PIECES):
                for k in range(KT):
                    last = mm(S[c][:, 0:PIECE], xT[:, k, 0:XCH, :].rearrange("p t b -> p (t b)"),
                              Wx[:, k, c * PIECE:(c + 1) * PIECE], start=k == 0, stop=k == KT - 1)
                last.then_inc(xp_mm, 1)
            pe.wait_ge(ready, 1)
            pe.wait_ge(xp_in[0], 16)
            inject(0)

            def quad(j):
                return slice(LANES * j, LANES * (j + 1))

            def rounded_scores(bank, j, c, nb, total):
                last = mm(bank[:, 0:nb * BLOCK], q_r[quad(j), :], k_r[quad(j), c * BLOCK:(c + nb) * BLOCK],
                          start=True, stop=c + nb < total, skip_group_check=True, tile_position=(LANES * j, 0))
                if c + nb == total:
                    last = mm(bank[:, (nb - 1) * BLOCK:nb * BLOCK], identh[:, :], tri_h[:, :], start=False, stop=True,
                              skip_group_check=True)
                return last

            def scores_t(c, j, total):
                for kb in range(c, min(c + CHUNK, total)):
                    o = S[j][:, (kb - c) * BLOCK:(kb - c + 1) * BLOCK]
                    last = mm(o, kst[:, kb * BLOCK:(kb + 1) * BLOCK], q_head[:, j, :], start=True,
                              stop=kb != total - 1, skip_group_check=True)
                    if kb == total - 1:
                        last = mm(o, identh[:, :], tri_th[:, :], start=False, stop=True, skip_group_check=True)
                last.then_inc(p2_ready[c // CHUNK], 1)

            def image_scores_t():
                o = misc[0:QUADS, 0:BLOCK]
                mm(o, kimg_st[:, :], qT[:, :], start=True, stop=False)
                mm(o, MT[:, MAX_ROW::LANES], ident[:, :], start=False, stop=True).then_inc(misc_ready, 1)

            def values(blocks, total):
                for kb in blocks:
                    for j in range(QUADS):
                        last = mm(PV[quad(j), 0:BLOCK], vst[:, kb, quad(j)], PT[:, j, kb, :],
                                  start=False, stop=kb == total - 1, skip_group_check=True,
                                  tile_position=(0, LANES * j))
                return last

            def body(ph, n, lstm, new, old):
                t = BLOCK * ph + STEPS * n
                T = tiles_before(ph, n)
                cur, B = (ph - 1) % 2, ph
                Bold = ph if inner(n) else ph - 1
                mask_at = (B - 1) * BLOCK

                def open_misc(name):
                    wait(pe, misc_free, misc_use(ph, n, new, old, name))

                def image_products():
                    pe.wait_ge(loaded, 16 * len(REST))
                    pe.wait_ge(masks_made, 1)
                    for i, (w, bias) in enumerate(((Wuk, Buk), (Wuv, Buv))):
                        for tile in range(TILES):
                            at = (i * TILES + tile) * BATCH
                            o = misc[:, at:at + BATCH]
                            for k in range(KT):
                                mm(o, w[:, k, tile, :], condT[:, k, :], start=k == 0, stop=False, skip_group_check=True)
                            last = mm(o, bias[:, tile, :], ones_mask[0:1, 0, 0:BATCH], start=False, stop=True,
                                      skip_group_check=True)
                    last.then_inc(img_mm, 1)

                def scores_for_max(half, heads):
                    c, nb = chunks(B)[half]
                    for j in heads:
                        if half:
                            pe.wait_ge(max0_done, QUADS * late_tiles_before(ph, n) + j + 1)
                        else:
                            wait_scores_read(pe, ph, n, j)
                        rounded_scores(S[j], j, c, nb, B).then_inc(p1_ready[half], 1)

                def fillers(st):
                    if B > CHUNK:
                        return 0
                    return int(st in (0, 1, 8, 9, 14, 15) or (B == 1 and st in (10, 11, 12, 13)))

                def keep_warm():
                    bank = S[0] if st in (8, 9) else PV
                    mm(bank[:, P:2 * P], ident[:, :], tri[:, :], start=True, stop=True, skip_group_check=True)

                for st in range(STEPS):
                    if lstm:
                        for k in range(KT):
                            pe.wait_ge(h_done[k], t + st + 1)
                            for b in range(KT):
                                last = group(b, ring[:, (st - 1) % STEPS, k, :], Wh[:, k], False, k == KT - 1)
                                if k == KT - 1:
                                    last.then_inc(g_ready[b], 1)
                    first = ph == 1 and not inner(n)
                    if first and st == 0:
                        image_products()
                    if first and st in (7, 8):
                        pe.wait_ge(img_made, st - 6)
                        for tile in range(TILES):
                            last = mm(PV[0:QUADS, tile * P:(tile + 1) * P], VIMG_T[:, (st - 7) * TILES + tile, :],
                                      ident[:, :], start=True, stop=True, skip_group_check=True)
                        last.then_inc(img_mm, 1)
                    if st in (0, 1) and old and Bold > CHUNK:
                        pe.wait_ge(exp_done[0], QUADS * (T - 1) + 2 + st + 1)
                        scores_t(CHUNK, 2 + st, Bold)
                    if ph == 0:
                        i, k = divmod(st, KT)
                        u, c = divmod(i, PIECES)
                        if k == 0:
                            if c == 0:
                                pe.wait_ge(x_in[u], 16 * (n + 1))
                            pe.wait_ge(xp_add, PIECES * 2 * n + i + 1)
                        last = mm(S[c][:, 0:PIECE], x_st[:, u, k, :], Wx[:, k, c * PIECE:(c + 1) * PIECE],
                                  start=k == 0, stop=k == KT - 1)
                        if k == KT - 1:
                            last.then_inc(xp_mm, 1)
                    if st in (2, 3) and new:
                        which = st - 2
                        open_misc("k" if which else "q")
                        if first and not which:
                            pe.wait_ge(img_copied, 1)
                        if not which:
                            pe.wait_ge(wst_in, 16 * (T + 1))
                            pe.wait_ge(bst_ready, T + 1)
                            pe.wait_ge(x1_evac, 2 * BODIES * ph)
                        for k in range(KT):
                            mm(misc[:, 0:BLOCK], wst[:, which, k, :], X1[cur][:, k, n // TILES, :], start=k == 0, stop=False)
                        mm(misc[:, 0:BLOCK], bst[:, which, :], ones_mask[:, n // TILES, mask_at:mask_at + BLOCK],
                           start=False, stop=True).then_inc(misc_ready, 1)
                    if st == 4 and new:
                        open_misc("img1")
                        pe.wait_ge(kimg_ready, T + 1)
                        mm(misc[:, 0:QUADS], qT[:, :], kimg_st[:, :], start=True, stop=True).then_inc(misc_ready, 1)
                        if B > 1:
                            pe.wait_ge(k_rounded, T - BODIES + 1)
                    if new and st in (4, 5, 6):
                        last_two = {5: (2,), 6: (3,)} if B > CHUNK else {5: (), 6: (2, 3)}
                        scores_for_max(0, (0, 1) if st == 4 else last_two[st])
                    if new and st in (6, 7, 8) and B > CHUNK:
                        scores_for_max(1, {6: (0, 1), 7: (2,), 8: (3,)}[st])
                    if st == 5 and new:
                        open_misc("v")
                        pe.wait_ge(x1st_in, 16 * (T + 1))
                        for k in range(KT):
                            mm(misc[:, 0:P], x1st[:, k, :], Wv[:, k, n % TILES, :], start=k == 0, stop=False)
                        mm(misc[:, 0:P], ones_mask[0:1, 0, 0:BLOCK], Bv[:, n % TILES, :], start=False,
                           stop=True).then_inc(misc_ready, 1)
                    if st == 6 and new and not inner(n):
                        open_misc("init")
                        for b in range(BATCH):
                            for k in range(KT):
                                lo = b * D + k * P
                                last = nc.tensor.transpose(misc[:, lo:lo + P], X1[cur][:, k, b, :], ident[:, :])
                        last.then_inc(misc_ready, 1)
                    if old and st in (7, 8, 9):
                        lo, hi = {7: (0, 2), 8: (2, 5), 9: (5, 8)}[st]
                        some = range(lo, min(hi, Bold))
                        if st == 7:
                            pe.wait_ge(vimg_ready, T)
                            pe.wait_ge(misc_free, misc_use(ph, n, new, old, "q" if new else "sel"))
                            mm(PV[:, 0:BLOCK], vimg_st[:, :], PTi[:, :], start=True, stop=False,
                               skip_group_check=True).then_inc(vimg_used, 1)
                            pe.wait_ge(exp_done[0], QUADS * T)
                            pe.wait_ge(vst_in, 16 * T)
                        if st == 8 and Bold > CHUNK:
                            pe.wait_ge(exp_done[1], QUADS * late_tiles_before(ph, n))
                        if some:
                            last = values(some, Bold)
                            if some[-1] == Bold - 1:
                                last.then_inc(pv_ready, 1)
                    if st == 9 and new:
                        open_misc("max")
                        pe.wait_ge(mt_done, T + 1)
                        nc.tensor.transpose(misc[:, 0:P], MT[:, :], ident[:, :]).then_inc(misc_ready, 1)
                    if new and st in (10, 11, 12, 13):
                        if st == 10:
                            pe.wait_ge(misc_free, misc_use(ph, n, new, old, "max") + 1)
                        scores_t(0, st - 10, B)
                    if st == 10 and old:
                        open_misc("sel")
                        pe.wait_ge(oT_ready, T)
                        mm(misc[:, 0:BLOCK], sel[:, :], oT[:, :], start=True, stop=True).then_inc(misc_ready, 1)
                    if st == 14 and old:
                        open_misc("proj")
                        pe.wait_ge(OT_ready, T)
                        tile = (n - 1) % TILES if inner(n) else TILES - 1
                        mm(misc[:, 0:D], OT[:, :], Wp[:, tile, :], start=True, stop=True).then_inc(misc_ready, 1)
                    if st == 15 and new:
                        open_misc("img2")
                        image_scores_t()
                    if new and st in (14, 15) and B > CHUNK:
                        pe.wait_ge(exp_done[0], QUADS * T + st - 14 + 1)
                        scores_t(CHUNK, st - 14, B)
                    for _ in range(fillers(st) if lstm and new else 0):
                        keep_warm()
                    if lstm:
                        nxt = (st + 1) % STEPS
                        if nxt == 0:
                            pe.wait_ge(xp_in[0], 16 * (BODIES * ph + n + 2))
                        if nxt == STEPS // 2:
                            pe.wait_ge(xp_in[1], 16 * (BODIES * ph + n + 1))
                        for b in range(KT):
                            pe.wait_ge(t_done[b], t + st + 1)
                        inject(nxt)

            bodies(pe, body)

            def last_body(n, start, before):
                T = BEFORE + n
                late = T - BODIES * CHUNK
                m = n + 1
                block_keys = slice(SEQ - BLOCK, SEQ)
                X = X1[(PHASES - 1) % 2]

                def open_misc(name):
                    pe.wait_ge(misc_free, last_use(n, name))

                def project(name, i):
                    open_misc(name)
                    pe.wait_ge(wst_in, 16 * (T + 2))
                    pe.wait_ge(bst_ready, T + 2)
                    for k in range(KT):
                        mm(misc[:, 0:BLOCK], wst[:, i, k, :], X[:, k, m // TILES, :], start=k == 0, stop=False)
                    mm(misc[:, 0:BLOCK], bst[:, i, :], ones_mask[:, m // TILES, block_keys],
                       start=False, stop=True).then_inc(misc_ready, 1)

                def image_scores():
                    open_misc("img1")
                    pe.wait_ge(kimg_ready, T + 2)
                    mm(misc[:, 0:QUADS], qT[:, :], kimg_st[:, :], start=True, stop=True).then_inc(misc_ready, 1)

                def for_max(*units):
                    for u in units:
                        half, j = divmod(u, QUADS)
                        if u == 0:
                            pe.wait_ge(k_rounded, T + 2 - BODIES)
                        if u >= 2 or not lead(n):
                            pe.wait_ge(last_max, 2 * QUADS * m + u - 1)
                        rounded_scores(gp[u % 2], j, half * CHUNK, CHUNK, PHASES).then_inc(last_scores, 1)

                def own_values():
                    open_misc("v")
                    pe.wait_ge(x1st_in, 16 * (T + 2))
                    for k in range(KT):
                        mm(misc[:, 0:P], x1st[:, k, :], Wv[:, k, m % TILES, :], start=k == 0, stop=False)
                    mm(misc[:, 0:P], ones_mask[0:1, 0, 0:BLOCK], Bv[:, m % TILES, :], start=False,
                       stop=True).then_inc(misc_ready, 1)

                def maxima_to_rows():
                    open_misc("max")
                    pe.wait_ge(mt_done, T + 2)
                    nc.tensor.transpose(misc[:, 0:P], MT[:, :], ident[:, :]).then_inc(misc_ready, 1)

                if not lead(n):
                    queries_in = last_use(n - 1 if isinstance(n, int) else n, "max") + 1 - (0 if isinstance(n, int) else 8)

                def p2(c, j):
                    if c == 0:
                        pe.wait_ge(exp_done[1], QUADS * (late - 1) + j + 1)
                        if j == 0:
                            pe.wait_ge(kst_half_in[0], 16 * (n + 1))
                            pe.wait_ge(misc_free, queries_in)
                    else:
                        pe.wait_ge(exp_done[0], QUADS * T + j + 1)
                        if j == 0:
                            pe.wait_ge(kst_half_in[1], 16 * (n + 1))
                    scores_t(c * CHUNK, j, PHASES)

                def output_product(name, tile, count):
                    open_misc(name)
                    pe.wait_ge(OT_ready, count)
                    mm(misc[:, 0:D], OT[:, :], Wp[:, tile % TILES, :], start=True, stop=True).then_inc(misc_ready, 1)

                if lead(n):
                    project("q", 0)
                    project("k", 1)
                    image_scores()
                    for_max(0, 1)
                    own_values()
                    for_max(2, 3, 4, 5)
                    open_misc("init")
                    for b in range(BATCH):
                        for k in range(KT):
                            lo = b * D + k * P
                            last = nc.tensor.transpose(misc[:, lo:lo + P], X[:, k, b, :], ident[:, :])
                    last.then_inc(misc_ready, 1)
                    for_max(6, 7)
                    maxima_to_rows()
                    return
                p2(0, 0)
                open_misc("img2")
                image_scores_t()
                p2(0, 1)
                if start:
                    project("q", 0)
                p2(0, 2)
                if before:
                    output_product("proj", n - 1, T)
                if start:
                    project("k", 1)
                p2(0, 3)
                if start:
                    image_scores()
                    for_max(0, 1)
                p2(1, 0)
                if start:
                    for_max(2)
                    own_values()
                p2(1, 1)
                if start:
                    for_max(3, 4)
                p2(1, 2)
                if start:
                    for_max(5)
                p2(1, 3)
                if start:
                    for_max(6)
                pe.wait_ge(vimg_ready, T + 1)
                pe.wait_ge(misc_free, last_use(n, "img2") + 1)
                mm(PV[:, 0:BLOCK], vimg_st[:, :], PTi[:, :], start=True, stop=False,
                   skip_group_check=True).then_inc(vimg_used, 1)
                pe.wait_ge(vst_in, 16 * (T + 1))
                values(range(0, CHUNK), PHASES)
                if start:
                    for_max(7)
                pe.wait_ge(exp_done[1], QUADS * (late + 1))
                values(range(CHUNK, PHASES), PHASES).then_inc(pv_ready, 1)
                if start:
                    maxima_to_rows()
                open_misc("sel")
                pe.wait_ge(oT_ready, T + 1)
                mm(misc[:, 0:BLOCK], sel[:, :], oT[:, :], start=True, stop=True).then_inc(misc_ready, 1)
                if not start:
                    output_product("end", n, T + 1)

            last_bodies(pe, last_body)

        @block.scalar
        def _(act):
            act.wait_ge(ready, 1)
            nc.scalar.activation(TC[0][:, :], condT[:, 0, :], ACT.Tanh)

            def body(ph, n, lstm, new, old):
                t = BLOCK * ph + STEPS * n
                T = tiles_before(ph, n)
                B = ph
                Bold = ph if inner(n) else ph - 1

                def exp(c, j, total, count):
                    nb = min(CHUNK, total - c)
                    act.wait_ge(p2_ready[c // CHUNK], count)
                    nc.scalar.activation(PT[:, j, c:c + nb, :].rearrange("p k q -> p (k q)"),
                                         S[j][:, 0:nb * BLOCK], ACT.Exp).then_inc(exp_done[c // CHUNK], 1)

                for st in range(STEPS):
                    now, nxt = st % 2, (st + 1) % 2
                    if lstm:
                        def tanh_gates(b, lo, hi, ready, done):
                            act.wait_ge(ready[b], t + st + 1)
                            nc.scalar.activation(
                                G[b][:, now, :, lo:hi].rearrange("p r g -> p g r"),
                                Tsb[b][:, :].rearrange("p (g r) -> p g r", g=GATES)[:, lo:hi, 0:BATCH],
                                ACT.Tanh).then_inc(done[b], 1)

                        def tanh_c(b):
                            act.wait_ge(c_done[b], t + st + 1)
                            nc.scalar.activation(TC[b][:, :], G[b][:, nxt, :, C_AT], ACT.Tanh).then_inc(tc_done[b], 1)

                        tanh_gates(0, 0, O_AT, ifg_done, th_done)
                        tanh_gates(0, O_AT, GATES, t_done, tho_done)
                        tanh_gates(1, 0, O_AT, ifg_done, th_done)
                        tanh_c(0)
                        tanh_gates(1, O_AT, GATES, t_done, tho_done)
                        tanh_c(1)
                    if ph == 1 and not inner(n) and st == 0:
                        act.wait_ge(img_mm, 1)
                        nc.scalar.activation(img[:, :, :].rearrange("p i (b t) -> p i t b", b=BATCH),
                                             misc[:, 0:2 * BODIES].rearrange("p (i t b) -> p i t b", i=2, b=BATCH),
                                             ACT.Copy).then_inc(img_copied, 1)
                    if st in (0, 1) and old and Bold > CHUNK:
                        exp(CHUNK, 2 + st, Bold, QUADS * (late_tiles_before(ph, n) - 1) + 2 + st + 1)
                    if st == 2 and new:
                        act.wait_ge(misc_ready, misc_use(ph, n, new, old, "q") + 1)
                        nc.scalar.activation(q_r[:, :], misc[:, 0:BLOCK], ACT.Copy, scale=SCALE)
                        nc.scalar.activation(qT[:, :], misc[:, 0:BLOCK], ACT.Copy, scale=SCALE).then_inc(misc_free, 1)
                    if st == 3 and new:
                        act.wait_ge(misc_ready, misc_use(ph, n, new, old, "k") + 1)
                        wait(act, k_stored, 16 * T if B < PHASES else 16 * BODIES * (PHASES - 1))
                        nc.scalar.activation(k_r[:, (B - 1) * BLOCK:B * BLOCK], misc[:, 0:BLOCK], ACT.Copy)
                        nc.scalar.activation(kst[:, (B - 1) * BLOCK:B * BLOCK], misc[:, 0:BLOCK],
                                             ACT.Copy).then_inc(misc_free, 1)
                    if st == 5 and new:
                        act.wait_ge(misc_ready, misc_use(ph, n, new, old, "v") + 1)
                        nc.scalar.activation(kv_all[:, n, SEQ + (B - 1) * P:SEQ + B * P], misc[:, 0:P],
                                             ACT.Copy).then_inc(misc_free, 1)
                    if st == 9 and old:
                        act.wait_ge(pv_ready, T)
                        nc.scalar.activation(oT[:, :], PV[:, 0:BLOCK], ACT.Copy).then_inc(oT_ready, 1)
                    if st in (10, 11, 12, 13) and new:
                        exp(0, st - 10, B, QUADS * T + st - 10 + 1)
                    if st in (14, 15) and new and B > CHUNK:
                        exp(CHUNK, st - 14, B, QUADS * late_tiles_before(ph, n) + st - 14 + 1)
                    if st == 15 and new:
                        act.wait_ge(misc_ready, misc_use(ph, n, new, old, "img2") + 1)
                        nc.scalar.activation(PTi[:, :], misc[0:QUADS, 0:BLOCK], ACT.Exp).then_inc(misc_free, 1)

            bodies(act, body)

            def last_body(n, start, before):
                T = BEFORE + n
                late = T - BODIES * CHUNK
                m = n + 1

                def exp(c, j):
                    act.wait_ge(p2_ready[c], QUADS * (late if c else T) + j + 1)
                    nc.scalar.activation(PT[:, j, c * CHUNK:(c + 1) * CHUNK, :].rearrange("p k q -> p (k q)"),
                                         S[j][:, :], ACT.Exp).then_inc(exp_done[c], 1)

                def take_q():
                    act.wait_ge(misc_ready, last_use(n, "q") + 1)
                    nc.scalar.activation(q_r[:, :], misc[:, 0:BLOCK], ACT.Copy, scale=SCALE)
                    nc.scalar.activation(qT[:, :], misc[:, 0:BLOCK], ACT.Copy, scale=SCALE).then_inc(misc_free, 1)

                def take_k():
                    act.wait_ge(misc_ready, last_use(n, "k") + 1)
                    nc.scalar.activation(k_r[:, SEQ - BLOCK:], misc[:, 0:BLOCK], ACT.Copy)
                    nc.scalar.activation(kv_all[:, m, SEQ - BLOCK:SEQ], misc[:, 0:BLOCK], ACT.Copy).then_inc(misc_free, 1)

                def take_v():
                    act.wait_ge(misc_ready, last_use(n, "v") + 1)
                    nc.scalar.activation(kv_all[:, m, SEQ + (PHASES - 1) * P:], misc[:, 0:P],
                                         ACT.Copy).then_inc(misc_free, 1)

                if lead(n):
                    take_q()
                    take_k()
                    take_v()
                    return
                exp(0, 0)
                act.wait_ge(misc_ready, last_use(n, "img2") + 1)
                nc.scalar.activation(PTi[:, :], misc[0:QUADS, 0:BLOCK], ACT.Exp).then_inc(misc_free, 1)
                exp(0, 1)
                if start:
                    take_q()
                exp(0, 2)
                if start:
                    take_k()
                exp(0, 3)
                exp(1, 0)
                if start:
                    take_v()
                for j in (1, 2, 3):
                    exp(1, j)
                act.wait_ge(pv_ready, T + 1)
                nc.scalar.activation(oT[:, :], PV[:, 0:BLOCK], ACT.Copy).then_inc(oT_ready, 1)

            last_bodies(act, last_body)

        @block.vector
        def _(dve):
            v = nc.vector
            dve.wait_ge(loaded_first, 16 * len(FIRST))
            gates = Wx[:].rearrange("p k (m g c) -> p (k m) g c", g=GATES, c=LANES)
            for sigmoids in (slice(0, G_AT), slice(O_AT, GATES)):
                v.tensor_scalar(gates[:, :, sigmoids, :], gates[:, :, sigmoids, :], 0.5, None, ALU.mult)
            gates = bx[:, :].rearrange("p (m g c) -> p m g c", g=GATES, c=LANES)
            for sigmoids in (slice(0, G_AT), slice(O_AT, GATES)):
                last = v.tensor_scalar(gates[:, :, sigmoids, :], gates[:, :, sigmoids, :], 0.5, None, ALU.mult)
            last.then_inc(scaled, 1)
            dve.wait_ge(scaled, 1)
            for c in range(PIECES):
                dve.wait_ge(xp_mm, c + 1)
                cols = slice(c * PIECE, (c + 1) * PIECE)
                v.tensor_tensor(xps[:, cols], S[c][:, 0:PIECE], bx[:, cols], ALU.add).then_inc(xp_add, 1)
            gates = Wh[:].rearrange("p k (m g c) -> p (k m) g c", g=GATES, c=LANES)
            for sigmoids in (slice(0, G_AT), slice(O_AT, GATES)):
                v.tensor_scalar(gates[:, :, sigmoids, :], gates[:, :, sigmoids, :], 0.25, None, ALU.mult)
            v.tensor_scalar(gates[:, :, G_AT, :], gates[:, :, G_AT, :], 0.5, None, ALU.mult)
            for b in range(KT):
                v.memset(xp_st[b][:, :], 0.0)
                v.memset(gp[b][:, :], 0.0)
                v.memset(G[b][:, :, :, ONES_AT:ONES_AT + 2], 1.0)
                v.memset(G[b][:, 0, :, C_AT:C_AT + 1], 0.0)
            v.tensor_copy(pick[:, :], pickf[:, :])
            for k in range(KT):
                v.tensor_scalar(ring[:, STEPS - 1, k, :], condT[:, k, :], 2.0, None, ALU.mult).then_inc(h_done[k], 1)
            v.memset(q_head[:, :, :], 0.0)
            v.memset(MT[:, :], 0.0).then_inc(ready, 1)
            dve.wait_ge(loaded, 16 * len(REST))
            v.tensor_copy(identh[:, :], ident[:, :])
            v.tensor_copy(tri_h[:, :], tri[:, :])
            v.tensor_copy(tri_th[:, :], tri_t[:, :]).then_inc(masks_made, 1)

            def per_head(i):
                return (img[:, i, :].unsqueeze(2).to_broadcast([P, BODIES, QUADS]),
                        headc[:, :].unsqueeze(1).to_broadcast([P, BODIES, QUADS]))

            def body(ph, n, lstm, new, old):
                t = BLOCK * ph + STEPS * n
                T = tiles_before(ph, n)
                cur, B = (ph - 1) % 2, ph

                def maxima(c, j):
                    at = 1 + c // CHUNK
                    return v.reduce_max(mx[:, j, at:at + 1], S[j][:, 0:min(CHUNK, B - c) * BLOCK], AX)

                for st in range(STEPS):
                    now, nxt = st % 2, (st + 1) % 2
                    if lstm:
                        def transpose(b, lo, hi, done):
                            cols = slice(lo * LANES, hi * LANES)
                            v.transpose(Tsb[b][:, cols], gp[b][:, cols]).then_inc(done[b], 1)

                        def new_c(b):
                            dve.wait_ge(th_done[b], t + st + 1)
                            for r in range(BATCH):
                                last = v.tensor_tensor_reduce(
                                    out=products[b][:, r, :].rearrange("p (a k) -> p a k", a=2),
                                    in0=G[b][:, now, r, :].rearrange("p (a k) -> p a k", a=2)[:, :, 0:2],
                                    in1=G[b][:, now, r, G_AT:C_AT + 1:C_AT - G_AT].unsqueeze(1).to_broadcast([P, 2, 2]),
                                    scale=0.5, scalar=0.0, op0=ALU.mult, op1=ALU.add,
                                    accum_out=G[b][:, nxt, r, C_AT:C_AT + 1])
                            last.then_inc(c_done[b], 1)

                        dve.wait_ge(g_ready[0], t + st + 1)
                        transpose(0, 0, O_AT, ifg_done)
                        transpose(0, O_AT, GATES, t_done)
                        dve.wait_ge(g_ready[1], t + st + 1)
                        transpose(1, 0, O_AT, ifg_done)
                        new_c(0)
                        transpose(1, O_AT, GATES, t_done)
                        new_c(1)
                        for b in range(KT):
                            dve.wait_ge(tc_done[b], t + st + 1)
                            v.scalar_tensor_tensor(ring[:, st, b, :], G[b][:, now, :, O_AT], 1.0, TC[b][:, :],
                                                   ALU.add, ALU.mult).then_inc(h_done[b], 1)
                    first = ph == 1 and not inner(n)
                    if first and st == 1:
                        dve.wait_ge(img_copied, 1)
                        v.tensor_tensor(VIMG_T[:, :, :], *per_head(1), ALU.mult)
                        v.tensor_tensor(KIMG[:, :, :], *per_head(0), ALU.mult).then_inc(img_made, 1)
                    if first and st in (7, 8):
                        dve.wait_ge(img_mm, st - 5)
                        lo = (st - 7) * TILES
                        v.tensor_copy(VIMG[:, lo:lo + TILES, :],
                                      PV[0:QUADS, :].rearrange("p (t m) -> p t m", t=TILES)).then_inc(img_made, 1)
                    if ph == 0 and st % KT == KT - 1:
                        i = st // KT
                        cols = slice(i % PIECES * PIECE, (i % PIECES + 1) * PIECE)
                        dve.wait_ge(xp_mm, PIECES * (2 * n + 1) + i + 1)
                        dve.wait_ge(xp_split, 4 * (PIECES * (2 * n) + i + 1))
                        v.tensor_tensor(xps[:, cols], S[i % PIECES][:, 0:PIECE], bx[:, cols], ALU.add).then_inc(xp_add, 1)
                    if st == 4 and new:
                        dve.wait_ge(p1_ready[0], QUADS * T + 1)
                        dve.wait_ge(misc_ready, misc_use(ph, n, new, old, "img1") + 1)
                        v.tensor_copy(mx[:, :, 0], misc[:, 0:QUADS]).then_inc(misc_free, 1)
                    if st in (5, 6, 7) and new:
                        dve.wait_ge(p1_ready[0], QUADS * T + st - 4 + 1)
                    if st in (6, 7) and new and B > CHUNK:
                        dve.wait_ge(p1_ready[1], QUADS * late_tiles_before(ph, n) + st - 6 + 1)
                    if st in (4, 5, 6, 7) and new:
                        last = maxima(0, st - 4)
                        if B > CHUNK:
                            last.then_inc(max0_done, 1)
                        elif st == 7:
                            last.then_inc(max_done, 1)
                    if st in (6, 7) and new and B > CHUNK:
                        maxima(CHUNK, st - 6)
                    if st == 8 and new and B > CHUNK:
                        dve.wait_ge(p1_ready[1], QUADS * (late_tiles_before(ph, n) + 1))
                        for j in (2, 3):
                            last = maxima(CHUNK, j)
                        last.then_inc(max_done, 1)
                    if st == 6 and new and not inner(n):
                        dve.wait_ge(misc_ready, misc_use(ph, n, new, old, "init") + 1)
                        wait(dve, out_stored, 16 * BATCH * (ph - 2))
                        v.tensor_tensor(OUT[cur][:, :, :], misc[:, :].rearrange("p (b f) -> p b f", b=BATCH),
                                        bp[:, :].unsqueeze(1).to_broadcast([P, BATCH, D]), ALU.add).then_inc(misc_free, 1)
                    if lstm and st in (7, 15):
                        half = int(st == 15)
                        at = t + half * STEPS // 2
                        where = STEPS * n + half * STEPS // 2
                        for k in range(KT):
                            dve.wait_ge(h_done[k], at + STEPS // 2 + 1)
                        for b in range(BATCH):
                            last = v.scalar_tensor_tensor(
                                X1[ph % 2][:, :, b, bass.ds(where, STEPS // 2)],
                                ring[:, half * STEPS // 2:(half + 1) * STEPS // 2, :, b].rearrange("p t k -> p k t"), 0.5,
                                xT[:, :, bass.ds(at, STEPS // 2), b], ALU.mult, ALU.add)
                        last.then_inc(x1_evac, 1)
                    if st == 8 and new:
                        dve.wait_ge(max_done, T + 1)
                        parts = 2 + (B > CHUNK)
                        v.tensor_reduce(MT[:, MAX_ROW::LANES], mx[:, :, 0:parts], AX, ALU.max,
                                        negate=True).then_inc(mt_done, 1)
                    if st == 9 and new:
                        dve.wait_ge(misc_ready, misc_use(ph, n, new, old, "max") + 1)
                        for j in range(QUADS):
                            rows = slice(LANES * j, LANES * (j + 1))
                            last = v.tensor_tensor(q_head[rows, j, :], qT[rows, :], misc[rows, 0:BLOCK], ALU.add)
                        last.then_inc(misc_free, 1)
                    if st == 10 and old:
                        dve.wait_ge(misc_ready, misc_use(ph, n, new, old, "sel") + 1)
                        v.reciprocal(rec[:, 0:BLOCK // 2], misc[:, 0:BLOCK // 2])
                    if st == 11 and old:
                        v.reciprocal(rec[:, BLOCK // 2:], misc[:, BLOCK // 2:BLOCK]).then_inc(misc_free, 1)
                    if st == 12 and old:
                        dve.wait_ge(misc_free, misc_use(ph, n, new, old, "sel") + 1)
                        v.tensor_tensor(OT[:, :], oT[:, :], rec[:, :], ALU.mult).then_inc(OT_ready, 1)
                    if st == 14 and old:
                        o = OUT[cur][:, (n - 1) // TILES, :] if inner(n) else OUT[1 - cur][:, BATCH - 1, :]
                        dve.wait_ge(misc_ready, misc_use(ph, n, new, old, "proj") + 1)
                        v.tensor_tensor(o, o, misc[:, 0:D], ALU.add).then_inc(misc_free, 1)

            bodies(dve, body)

            def last_body(n, start, before):
                T = BEFORE + n
                m = n + 1
                rows_out = OUT[(PHASES - 1) % 2]

                def add_output(name, tile):
                    o = rows_out[:, tile // TILES, :]
                    dve.wait_ge(misc_ready, last_use(n, name) + 1)
                    v.tensor_tensor(o, o, misc[:, 0:D], ALU.add).then_inc(misc_free, 1)

                def image_maxima():
                    dve.wait_ge(misc_ready, last_use(n, "img1") + 1)
                    v.tensor_copy(mx[:, :, 0], misc[:, 0:QUADS]).then_inc(misc_free, 1)

                def maxima(*units):
                    for u in units:
                        half, j = divmod(u, QUADS)
                        dve.wait_ge(last_scores, 2 * QUADS * m + u + 1)
                        v.reduce_max(mx[:, j, 1 + half:2 + half], gp[u % 2][:, :], AX).then_inc(last_max, 1)

                def next_queries():
                    dve.wait_ge(last_max, 2 * QUADS * (m + 1))
                    v.tensor_reduce(MT[:, MAX_ROW::LANES], mx[:, :, :], AX, ALU.max, negate=True).then_inc(mt_done, 1)
                    dve.wait_ge(misc_ready, last_use(n, "max") + 1)
                    for j in range(QUADS):
                        rows = slice(LANES * j, LANES * (j + 1))
                        last = v.tensor_tensor(q_head[rows, j, :], qT[rows, :], misc[rows, 0:BLOCK], ALU.add)
                    last.then_inc(misc_free, 1)

                if lead(n):
                    image_maxima()
                    maxima(*range(6))
                    dve.wait_ge(misc_ready, last_use(n, "init") + 1)
                    dve.wait_ge(out_stored, 16 * BATCH * (PHASES - 2))
                    v.tensor_tensor(rows_out[:, :, :], misc[:, :].rearrange("p (b f) -> p b f", b=BATCH),
                                    bp[:, :].unsqueeze(1).to_broadcast([P, BATCH, D]), ALU.add).then_inc(misc_free, 1)
                    maxima(6, 7)
                    next_queries()
                    return
                if before:
                    add_output("proj", n - 1)
                if start:
                    image_maxima()
                    maxima(*range(2 * QUADS))
                    next_queries()
                dve.wait_ge(misc_ready, last_use(n, "sel") + 1)
                v.reciprocal(rec[:, :], misc[:, 0:BLOCK]).then_inc(misc_free, 1)
                dve.wait_ge(misc_free, last_use(n, "sel") + 1)
                v.tensor_tensor(OT[:, :], oT[:, :], rec[:, :], ALU.mult).then_inc(OT_ready, 1)
                if not start:
                    add_output("end", n)

            last_bodies(dve, last_body)


def _positions():
    import numpy as np
    feature = np.array([[64 * (q // 32) + 32 * k + q % 32 for q in range(128)] for k in range(2)])
    column = np.array([256 * g + 64 * j + 32 * b + p
                       for j in range(4) for b in range(2) for g in (0, 1, 3, 2) for p in range(32)])
    return feature, column


def kernel(**inputs):
    import numpy as np
    import concourse.bacc as _bacc
    from concourse import mybir as _mybir
    from concourse.bass_utils import run_bass_kernel_spmd as _run

    g = {k: np.asarray(v) for k, v in inputs.items()}
    feature, column = _positions()

    def by_feature(w):
        return w[feature].transpose(1, 0, *range(2, w.ndim + 1))

    def in_slots(w, ones=()):
        w = w.reshape(*w.shape[:-1], TILES, QUADS, HDIM)
        padded = np.zeros((*w.shape[:-1], LANES), np.float32)
        padded[..., :HDIM] = w
        for at, value in ones:
            padded[..., at] = value
        return padded.reshape(*w.shape[:-3], TILES, P)

    c_w, c_b = g["L1_cond_c_attn_w"], g["L1_cond_c_attn_b"]
    w_qk = np.stack([in_slots(by_feature(c_w[:, i * D:(i + 1) * D])) for i in range(2)], 1)
    b_q = in_slots(c_b[0:D], [(MASK_ROW, 1 / SCALE)])
    b_k = in_slots(c_b[D:2 * D], [(MAX_ROW, 1.0)])
    mask_slot = in_slots(np.zeros(D, np.float32), [(MASK_ROW, 1.0)])
    b_qk = np.stack([np.stack([b_q, b_k], 1), np.stack([np.zeros_like(b_q), mask_slot], 1)])
    rows = in_slots(np.ascontiguousarray(g["L1_cond_c_proj_w"].T)).transpose(2, 1, 0)
    block = np.arange(P) // LANES
    arrays = {
        "x_t": by_feature(g["x"].transpose(2, 1, 0)),
        "wx": by_feature(g["L0_cond_Wx"][:, column]),
        "wh": by_feature(g["L0_cond_Wh"][:, column]),
        "b_x": g["L0_cond_b"][column],
        "h0": by_feature(g["cond_1024"].T),
        "w_qk": w_qk.transpose(0, 3, 1, 2, 4),
        "b_qk": b_qk,
        "w_v": in_slots(by_feature(c_w[:, 2 * D:])),
        "b_v": in_slots(c_b[2 * D:], [(HDIM, 1.0)])[None],
        "w_p": rows[:, :, feature.reshape(-1)],
        "b_p": g["L1_cond_c_proj_b"][feature.reshape(-1)],
        "w_uk": in_slots(by_feature(g["L1_cond_uk_w"].T)),
        "b_uk": in_slots(g["L1_cond_uk_b"], [(MAX_ROW, 1.0)])[None],
        "w_uv": in_slots(by_feature(g["L1_cond_uv_w"].T)),
        "b_uv": in_slots(g["L1_cond_uv_b"], [(HDIM, 1.0)])[None],
        "mask": g["mask_Bx1x1xS_ff0"].reshape(1, BATCH, SEQ),
        "ident_in": np.eye(P, dtype=np.float32),
        "pick_in": ((np.arange(P)[:, None] % ROWS == np.arange(ROWS))
                    & (np.arange(P)[:, None] < PARTS * ROWS)).astype(np.float32),
        "sel_in": ((np.arange(P)[:, None] % LANES == HDIM) & (block[:, None] == block)).astype(np.float32),
        "tri_in": np.where(np.arange(P)[None] > np.arange(P)[:, None], np.float32(NEG), np.float32(0)),
        "tri_t_in": np.where(np.arange(P)[:, None] > np.arange(P)[None], np.float32(NEG), np.float32(0)),
        "head_col": (block[:, None] == np.arange(QUADS)).astype(np.float32),
    }
    arrays = {k: np.ascontiguousarray(v) for k, v in arrays.items()}
    nc = _bacc.Bacc("TRN2", target_bir_lowering=False, num_devices=1)
    args = {k: nc.dram_tensor(k, v.shape, _mybir.dt.float32, kind="ExternalInput").ap() for k, v in arrays.items()}
    out = nc.dram_tensor("out", (BATCH, SEQ, D), _mybir.dt.float32, kind="ExternalOutput").ap()
    lstm_attention(nc, **args, out=out)
    r = _run(nc, [arrays], core_ids=[0])
    rows = r.results[0]["out"]
    return rows.reshape(BATCH, SEQ, KT, QUADS, LANES).transpose(0, 1, 3, 2, 4).reshape(BATCH, SEQ, D)
```
